# Optimizing a Trainium2 kernel written in Bass

```python
import numpy as np
import jax
import jax.numpy as jnp

def _softmax(x, axis=-1):
    return jax.nn.softmax(x, axis=axis)

def _gelu(x):
    return jax.nn.gelu(x, approximate=True)

def _silu(x):
    return jax.nn.silu(x)

def _sigmoid(x):
    return jax.nn.sigmoid(x)

def _layernorm(x, axis=-1, eps=1e-05):
    m = jnp.mean(x, axis=axis, keepdims=True)
    v = jnp.var(x, axis=axis, keepdims=True)
    return (x - m) / jnp.sqrt(v + eps)

def _scatter_add(tgt, idx, src, axis=0):
    return tgt.at[idx].add(src)

def _segment_sum(src, seg, n):
    return jax.ops.segment_sum(src, seg, n)
kernel_name = 'mk_xattn_seq_d1_seqx_r2_5494d4'

def setup_inputs(seed: int=0):
    np.random.seed(seed)
    _w = jnp.asarray

    def _rec_inputs():
        import jax
        import jax.numpy as jnp
        _rk = jax.random.key(seed)
        x = -0.0002928 + 1 * jax.random.normal(jax.random.fold_in(_rk, 1), (8, 512, 512), jnp.float32)
        _lenS = 512 - jax.random.randint(jax.random.fold_in(_rk, 7), (8,), 0, max(1, 512 // 4) + 1, jnp.int32)
        _lenS2 = 120 - jax.random.randint(jax.random.fold_in(_rk, 8), (8,), 0, max(1, 120 // 4) + 1, jnp.int32)
        _ctx_1024P = jax.random.normal(jax.random.fold_in(_rk, 11), (8, 16, 512), jnp.float32)
        _ctx_1024c = jax.random.dirichlet(jax.random.fold_in(_rk, 511), 0.3 * jnp.ones((16,), jnp.float32), (8, 120))
        _ctx_1024t = jnp.einsum('bsk,bkd->bsd', _ctx_1024c, _ctx_1024P)
        _ctx_1024t = _ctx_1024t * jax.lax.rsqrt(jnp.mean(jnp.square(_ctx_1024t)) + 1e-12) * 0.953939
        ctx_1024 = -1.39393e-06 + 0.999914 * (_ctx_1024t + 0.3 * jax.random.normal(jax.random.fold_in(_rk, 611), (8, 120, 512), jnp.float32))
        return (x, ctx_1024)
    x, ctx_1024 = _rec_inputs()

    def _L0_xattn_setup():
        import jax, jax.numpy as jnp
        import numpy as np
        D = 512
        H = 16
        HD = D // H
        DFF = 4 * D
        LN_EPS = 1e-05

        def layernorm(x, gamma, beta):
            mu = jnp.mean(x, axis=-1, keepdims=True)
            var = jnp.mean(jnp.square(x - mu), axis=-1, keepdims=True)
            return (x - mu) * jax.lax.rsqrt(var + LN_EPS) * gamma + beta
        key = jax.random.key(seed)
        ks = jax.random.split(key, 10)
        B, Nq, Nk = (2, 1024, 1024)
        s = 0.02
        return {'q_x': jax.random.normal(ks[0], (B, Nq, D), jnp.float32), 'kv_x': jax.random.normal(ks[1], (B, Nk, D), jnp.float32), 'Wq': jax.random.normal(ks[2], (D, D), jnp.float32) * s, 'Wkv': jax.random.normal(ks[3], (2 * D, D), jnp.float32) * s, 'Wo': jax.random.normal(ks[4], (D, D), jnp.float32) * s, 'bo': jnp.zeros((D,), jnp.float32), 'ln_q_g': jnp.ones((D,), jnp.float32), 'ln_q_b': jnp.zeros((D,), jnp.float32), 'ln_kv_g': jnp.ones((D,), jnp.float32), 'ln_kv_b': jnp.zeros((D,), jnp.float32), 'W1': jax.random.normal(ks[5], (DFF, D), jnp.float32) * s, 'b1': jnp.zeros((DFF,), jnp.float32), 'W2': jax.random.normal(ks[6], (D, DFF), jnp.float32) * s, 'b2': jnp.zeros((D,), jnp.float32)}
    _L0_xattn_all = _L0_xattn_setup()
    _L0_xattn_in = {k: v for k, v in _L0_xattn_all.items() if k in ('Wq', 'Wkv', 'Wo', 'bo', 'ln_q_g', 'ln_q_b', 'ln_kv_g', 'ln_kv_b', 'W1', 'b1', 'W2', 'b2')}
    del _L0_xattn_all
    return {'x': x, 'ctx_1024': ctx_1024, 'L0_xattn_Wq': _L0_xattn_in['Wq'], 'L0_xattn_Wkv': _L0_xattn_in['Wkv'], 'L0_xattn_Wo': _L0_xattn_in['Wo'], 'L0_xattn_bo': _L0_xattn_in['bo'], 'L0_xattn_ln_q_g': _L0_xattn_in['ln_q_g'], 'L0_xattn_ln_q_b': _L0_xattn_in['ln_q_b'], 'L0_xattn_ln_kv_g': _L0_xattn_in['ln_kv_g'], 'L0_xattn_ln_kv_b': _L0_xattn_in['ln_kv_b'], 'L0_xattn_W1': _L0_xattn_in['W1'], 'L0_xattn_b1': _L0_xattn_in['b1'], 'L0_xattn_W2': _L0_xattn_in['W2'], 'L0_xattn_b2': _L0_xattn_in['b2']}

def reference(x, ctx_1024, L0_xattn_Wq, L0_xattn_Wkv, L0_xattn_Wo, L0_xattn_bo, L0_xattn_ln_q_g, L0_xattn_ln_q_b, L0_xattn_ln_kv_g, L0_xattn_ln_kv_b, L0_xattn_W1, L0_xattn_b1, L0_xattn_W2, L0_xattn_b2):
    import jax
    import jax.numpy as jnp

    def _L0_xattn_ref(q_x, kv_x, Wq, Wkv, Wo, bo, ln_q_g, ln_q_b, ln_kv_g, ln_kv_b, W1, b1, W2, b2):
        import jax, jax.numpy as jnp
        import numpy as np
        D = 512
        H = 16
        HD = D // H
        DFF = 4 * D
        LN_EPS = 1e-05

        def layernorm(x, gamma, beta):
            mu = jnp.mean(x, axis=-1, keepdims=True)
            var = jnp.mean(jnp.square(x - mu), axis=-1, keepdims=True)
            return (x - mu) * jax.lax.rsqrt(var + LN_EPS) * gamma + beta
        B, Nq, _ = q_x.shape
        Nk = kv_x.shape[1]
        scale = HD ** (-0.5)
        q = layernorm(q_x, ln_q_g, ln_q_b) @ Wq.T
        kv = layernorm(kv_x, ln_kv_g, ln_kv_b) @ Wkv.T
        q = q.reshape(B, Nq, H, HD).transpose(0, 2, 1, 3)
        kv = kv.reshape(B, Nk, 2, H, HD).transpose(2, 0, 3, 1, 4)
        k, v = (kv[0], kv[1])
        attn = jnp.einsum('bhqd,bhkd->bhqk', q, k) * scale
        attn = jax.nn.softmax(attn, axis=-1)
        out = jnp.einsum('bhqk,bhkd->bhqd', attn, v)
        out = out.transpose(0, 2, 1, 3).reshape(B, Nq, D)
        x = q_x + out @ Wo.T + bo
        h = jax.nn.silu(x @ W1.T + b1)
        x = x + h @ W2.T + b2
        return x
    x = _L0_xattn_ref(x, ctx_1024, L0_xattn_Wq, L0_xattn_Wkv, L0_xattn_Wo, L0_xattn_bo, L0_xattn_ln_q_g, L0_xattn_ln_q_b, L0_xattn_ln_kv_g, L0_xattn_ln_kv_b, L0_xattn_W1, L0_xattn_b1, L0_xattn_W2, L0_xattn_b2)
    return x

_drawn_inputs = setup_inputs


def setup_inputs(seed=0):
    import zlib

    import numpy as np

    out = dict(_drawn_inputs(seed))
    spreads = {'L0_xattn_bo': (0.0, 0.1),
     'L0_xattn_ln_q_g': (1.0, 0.6),
     'L0_xattn_ln_q_b': (0.0, 0.8),
     'L0_xattn_ln_kv_g': (1.0, 0.6),
     'L0_xattn_ln_kv_b': (0.0, 0.408),
     'L0_xattn_b1': (0.0, 0.1),
     'L0_xattn_b2': (0.0, 0.1)}
    factors = {'L0_xattn_Wq': 6.741}
    for name, (base, spread) in spreads.items():
        noise = np.random.default_rng([zlib.crc32(name.encode()), seed]).standard_normal(out[name].shape)
        drawn = base * np.exp(spread * noise) if base else spread * noise
        out[name] = jnp.asarray(drawn.astype(out[name].dtype))
    for name, factor in factors.items():
        out[name] = (out[name] * factor).astype(out[name].dtype)
    return out
```

```python
from contextlib import ExitStack

import concourse.bass as bass
from concourse import mybir

F32 = mybir.dt.float32
F32R = mybir.dt.float32r
ALU = mybir.AluOpType
ACT = mybir.ActivationFunctionType
AX = mybir.AxisListType

P = 128
B, NQ, D = 8, 512, 512
NK = 120
H, HD = 16, 32
DFF = 4 * D
KT = D // P
GH = P // HD
NG = H // GH
QT = NQ // P
FT = DFF // P
CB = 4
CHUNKS = B // CB
CTOK = CB * NK
SCALE = float(HD) ** -0.5
EPS = 1e-5
V_GQ, V_BQ, V_GK, V_BK, V_BO, V_B2, V_B1 = 0, KT, 2 * KT, 3 * KT, 4 * KT, 5 * KT, 6 * KT
NV = 6 * KT + FT

SLOTS = NG * QT
T_LAG = 6
PV_LAG = 10
OUT_STEP = {13: 0, 15: 1, 3: 2, 7: 3}
LN_SLOT = 0
LN_APPLY = 6
LNT_SLOT = 7
Q_NOW = {0: 2, 1: 2, 2: 2, 3: 2, 4: 1, 5: 1, 6: 2}
WO_BEFORE = {7: 3, 8: 3, 9: 2, 10: 3, 11: 3, 12: 2}
Q_NEXT = {13: 2, 14: 2}
Q_EVAC = {2: 1, 4: 2, 7: 3, 15: 0}
X2_EVAC = {9: 0, 10: 1, 12: 2, 13: 3}


def units(table, step, first_tile=0):
    done = sum(n for s, n in table.items() if s < step)
    return [divmod(first_tile * KT + done + j, KT) for j in range(table.get(step, 0))]


def cross_attention_block(nc, x, xT, ctx_in, wqT, wkT, wvT, woT, w1c, w2c, vecs, yT):
    k_scr = nc.dram_tensor("k_scratch", [2, B, P, NG, NK], F32).ap()
    v_scr = nc.dram_tensor("v_scratch", [B, P, D], F32).ap()
    x2_scr = nc.dram_tensor("x2_scratch", [B, KT, P, NQ], F32).ap()

    with ExitStack() as outer:
        def sem(name):
            return outer.enter_context(nc.semaphore(name))

        vec = outer.enter_context(nc.sbuf_tensor("vec", [P, NV], F32))
        bank = [outer.enter_context(nc.psum_tensor(f"bank{i}", [P, 512], F32)) for i in range(8)]

        early = ExitStack()

        def sb(name, shape, dt=F32):
            return early.enter_context(nc.sbuf_tensor(name, shape, dt))

        wq_hi, wq_lo = sb("wq_hi", [P, KT, D], F32R), sb("wq_lo", [P, KT, D], F32R)
        wo_hi, wo_lo = sb("wo_hi", [P, KT, D], F32R), sb("wo_lo", [P, KT, D], F32R)
        wk_hi, wk_lo = sb("wk_hi", [P, KT, D], F32R), sb("wk_lo", [P, KT, D], F32R)
        wv_hi, wv_lo = sb("wv_hi", [P, KT, D], F32R), sb("wv_lo", [P, KT, D], F32R)
        ident = sb("ident", [P, P])
        x_tok = sb("x_tok", [P, QT, D])
        stats = sb("stats", [P, QT, 6])
        mean_var = sb("mean_var", [P, QT, 2])
        eps, var_eps, minus_half, rstd = sb("eps", [P, QT]), sb("var_eps", [P, QT]), sb("minus_half", [P, QT]), sb("rstd", [P, QT])
        x_f = sb("x_f", [P, 2, NQ])
        xn_hi, xn_lo = sb("xn_hi", [P, KT, NQ], F32R), sb("xn_lo", [P, KT, NQ], F32R)
        q_hi, q_lo = sb("q_hi", [P, KT, NQ], F32R), sb("q_lo", [P, KT, NQ], F32R)
        o_hi, o_lo = sb("o_hi", [P, KT, NQ], F32R), sb("o_lo", [P, KT, NQ], F32R)
        kbd_hi, kbd_lo = sb("kbd_hi", [P, NG, GH * NK], F32R), sb("kbd_lo", [P, NG, GH * NK], F32R)
        k_out_hi, k_out_lo = sb("k_out_hi", [P, 2, CTOK], F32R), sb("k_out_lo", [P, 2, CTOK], F32R)
        v_now = sb("v_now", [P, D])
        probs = sb("probs", [P, 2, QT, GH * NK])
        probs_t = sb("probs_t", [P, 2 * GH, NQ])
        neg_max = sb("neg_max", [P, 2, QT * GH])
        row_sum = sb("row_sum", [P, 2, QT * GH])
        row_inv = sb("row_inv", [P, 2, QT * GH])
        xT_now = sb("xT_now", [P, KT, NQ])
        x2_out = sb("x2_out", [P, 2, NQ])
        early.close()

        late = ExitStack()
        outer.enter_context(late)

        def sl(name, shape, dt=F32):
            return late.enter_context(nc.sbuf_tensor(name, shape, dt))

        w1_hi, w1_lo = sl("w1_hi", [P, FT, KT * P], F32R), sl("w1_lo", [P, FT, KT * P], F32R)
        w2_hi, w2_lo = sl("w2_hi", [P, FT, D], F32R), sl("w2_lo", [P, FT, D], F32R)
        w_raw = sl("w_raw", [P, 2, 2, 512])
        x2_in = sl("x2_in", [P, KT, NQ])
        x2_res = sl("x2_res", [P, KT, NQ])
        x2_hi, x2_lo = sl("x2_hi", [P, KT, NQ], F32R), sl("x2_lo", [P, KT, NQ], F32R)
        h_f = sl("h_f", [P, 2, NQ])
        h_hi, h_lo = sl("h_hi", [P, 2, NQ], F32R), sl("h_lo", [P, 2, NQ], F32R)
        y_out = sl("y_out", [P, 2, NQ])

        raw_a = xT_now
        raw_b = probs[:, :, :, :].rearrange("p a t n -> p (a t n)")[:, 0:KT * D].rearrange("p (k n) -> p k n", k=KT)
        ctx_tok = [probs_t[0:NK, c * CB:(c + 1) * CB, :] for c in range(CHUNKS)]
        cn = [(o_hi, o_lo), (q_hi, q_lo)]
        v_out = x2_out

        ln_bank, proj, s_bank, t_bank, o_bank = bank[0], bank[1:3], bank[3:5], bank[5:7], bank[7]
        acc2 = [bank[0], bank[1], bank[2], bank[7]]
        acc1 = bank[3:7]

        vec_loaded, ident_zero, ident_ready, consts_ready, kbd_zero = sem("vec_loaded"), sem("ident_zero"), sem("ident_ready"), sem("consts_ready"), sem("kbd_zero")
        ctx_loaded = [sem(f"ctx_loaded{c}") for c in range(CHUNKS)]
        x_loaded, xT_loaded, v_loaded = sem("x_loaded"), sem("xT_loaded"), sem("v_loaded")
        kbd_loaded = [sem("kbd01_loaded"), sem("kbd23_loaded")]
        w_loaded = {n: sem(f"w{n}_loaded") for n in "kvqo"}
        w_hi_done = {n: sem(f"w{n}_hi_done") for n in "kvqo"}
        w_lo_done = {n: sem(f"w{n}_lo_done") for n in "kvqo"}
        k_stored = [sem("k_stored0"), sem("k_stored1")]
        stored = [sem("stored0"), sem("stored1")]
        V_STORES = 16 * B // 2
        X2_STORES = V_STORES + 16 * B * KT // 2
        Y_STORES = X2_STORES + 16 * B * KT // 2
        stats_step, aggregated, var_done, rstd_done, ln_done = sem("stats_step"), sem("aggregated"), sem("var_done"), sem("rstd_done"), sem("ln_done")
        lnt_ready, xf_done, xhi_done, xn_ready = sem("lnt_ready"), sem("xf_done"), sem("xhi_done"), sem("xn_ready")
        k_mm, v_mm, q_mm, wo_mm = sem("k_mm"), sem("v_mm"), sem("q_mm"), sem("wo_mm")
        khi_done, k_evac, v_evac = sem("khi_done"), sem("k_evac"), sem("v_evac")
        qhi_done, q_ready, x2_evac = sem("qhi_done"), sem("q_ready"), sem("x2_evac")
        s_ready, max_done, exp_done, inv_done, norm_done = (sem(n) for n in ("s_ready", "max_done", "exp_done", "inv_done", "norm_done"))
        t_ready, pt_ready, o_mm, ohi_done, o_ready = (sem(n) for n in ("t_ready", "pt_ready", "o_mm", "ohi_done", "o_ready"))
        attn_done = sem("attn_done")
        wraw_loaded, whi2_done, wlo2_done = [sem("wraw_loaded0"), sem("wraw_loaded1")], sem("whi2_done"), sem("wlo2_done")
        x2_loaded, x2hi_done, x2_split, res_ready = sem("x2_loaded"), sem("x2hi_done"), sem("x2_split"), sem("res_ready")
        f1_mm, silu_done, hhi_done, h_ready, f2_mm, y_done = (sem(n) for n in ("f1_mm", "silu_done", "hhi_done", "h_ready", "f2_mm", "y_done"))

        FIRST, LAST, TAIL = 0, B - 1, B

        def is_at(i, n):
            return isinstance(i, int) and i == n

        def each_batch(eng, step):
            step(FIRST)
            with eng.Fori(1, LAST) as i:
                step(i)
            step(LAST)
            step(TAIL)

        block = outer.enter_context(nc.Block())

        @block.sync
        def _(sp):
            sp.dma_start(ctx_tok[0], ctx_in[0:CTOK, :].rearrange("(t p) d -> p t d", p=NK)).then_inc(ctx_loaded[0], 16)
            sp.dma_start(raw_a[:, :, :], wkT.rearrange("(k p) n -> p k n", p=P)).then_inc(w_loaded["k"], 16)
            sp.dma_start(vec[:, :], vecs).then_inc(vec_loaded, 16)
            sp.dma_start(ctx_tok[1], ctx_in[CTOK:2 * CTOK, :].rearrange("(t p) d -> p t d", p=NK)).then_inc(ctx_loaded[1], 16)
            sp.dma_start(raw_b, wvT.rearrange("(k p) n -> p k n", p=P)).then_inc(w_loaded["v"], 16)
            sp.dma_start(x_tok[:, :, :], x[0].rearrange("(t p) d -> p t d", p=P)).then_inc(x_loaded, 16)
            sp.wait_ge(w_lo_done["k"], 1)
            sp.dma_start(raw_a[:, :, :], wqT.rearrange("(k p) n -> p k n", p=P)).then_inc(w_loaded["q"], 16)
            sp.wait_ge(w_lo_done["v"], 1)
            sp.dma_start(raw_b, woT.rearrange("(k p) n -> p k n", p=P)).then_inc(w_loaded["o"], 16)
            for c in range(CHUNKS):
                for g in range(NG):
                    sp.wait_ge(k_evac, c * NG + g + 1)
                    for part, src in enumerate((k_out_hi, k_out_lo)):
                        sp.dma_start(k_scr[part, c * CB:(c + 1) * CB, :, g, :].rearrange("b p n -> p b n"),
                                     src[:, g % 2, :].bitcast(F32).rearrange("p (b n) -> p b n", b=CB)).then_inc(k_stored[g % 2], 16)
                for b in range(CB):
                    sp.wait_ge(v_evac, c * CB + b + 1)
                    sp.dma_start(v_scr[c * CB + b, 0:NK], v_out[0:NK, b % 2, :]).then_inc(stored[b % 2], 16)

            def load_kbd(b, half):
                groups = slice(2 * half, 2 * half + 2)
                for part, dst in enumerate((kbd_hi, kbd_lo)):
                    for j in range(GH):
                        rows = slice(HD * j, HD * (j + 1))
                        sp.dma_start(dst[rows, groups, j * NK:(j + 1) * NK].bitcast(F32),
                                     k_scr[part, b, rows, groups, :]).then_inc(kbd_loaded[half], 16)

            for s in range(2):
                sp.wait_ge(k_stored[s], 16 * 2 * NG // 2 * CHUNKS)
                sp.wait_ge(stored[s], V_STORES)
            sp.wait_ge(kbd_zero, 2)
            load_kbd(0, 0)
            load_kbd(0, 1)

            def batch(i):
                first, tail = is_at(i, FIRST), is_at(i, TAIL)
                if not tail and not is_at(i, LAST):
                    sp.wait_ge(lnt_ready, (i + CHUNKS + 1) * KT)
                    sp.dma_start(x_tok[:, :, :], x[i + 1].rearrange("(t p) d -> p t d", p=P)).then_inc(x_loaded, 16)
                if not first:
                    if not tail:
                        sp.wait_ge(s_ready, i * SLOTS)
                        load_kbd(i, 1)
                    sp.wait_ge(stored[1], V_STORES + 16 * KT // 2 * (i - 1))
                    sp.dma_start(xT_now[:, :, :], xT[i - 1]).then_inc(xT_loaded, 16)
                if not tail:
                    if not first:
                        sp.wait_ge(o_mm, i * NG)
                    sp.dma_start(v_now[0:NK, :], v_scr[i, 0:NK]).then_inc(v_loaded, 16)
                if not tail and not is_at(i, LAST):
                    sp.wait_ge(s_ready, i * SLOTS + 2 * QT)
                    load_kbd(i + 1, 0)
                if not first:
                    for m in range(KT):
                        sp.wait_ge(x2_evac, (i - 1) * KT + m + 1)
                        sp.dma_start(x2_scr[i - 1, m], x2_out[:, m % 2, :]).then_inc(stored[m % 2], 16)

            sp.wait_ge(w_lo_done["q"], 1)
            each_batch(sp, batch)

            for s in range(2):
                sp.wait_ge(stored[s], X2_STORES)
            sp.wait_ge(attn_done, 4)
            sp.dma_start(x2_in[:, :, :], x2_scr[0].rearrange("k p n -> p k n")).then_inc(x2_loaded, 16)
            for m in range(FT):
                if m >= 2:
                    sp.wait_ge(wlo2_done, m - 1)
                sp.dma_start(w_raw[:, m % 2, 0, :], w1c[m]).then_inc(wraw_loaded[m % 2], 16)
                sp.dma_start(w_raw[:, m % 2, 1, :], w2c[m]).then_inc(wraw_loaded[m % 2], 16)

            def keep_residual(b):
                sp.wait_ge(x2_split, (b + 1) * KT)
                sp.dma_start(x2_res[:, :, :], x2_in[:, :, :]).then_inc(res_ready, 16)

            def store_y(b):
                for m in range(KT):
                    sp.wait_ge(y_done, b * KT + m + 1)
                    sp.dma_start(yT[b, m], y_out[:, m % 2, :]).then_inc(stored[m % 2], 16)

            keep_residual(0)
            with sp.Fori(1, B) as b:
                sp.wait_ge(res_ready, 16 * b)
                sp.dma_start(x2_in[:, :, :], x2_scr[b].rearrange("k p n -> p k n")).then_inc(x2_loaded, 16)
                store_y(b - 1)
                keep_residual(b)
            store_y(B - 1)
            for s in range(2):
                sp.wait_ge(stored[s], Y_STORES)

        @block.gpsimd
        def _(pool):
            pool.memset(ident[:, :], 0.0).then_inc(ident_zero, 1)
            pool.wait_ge(ident_zero, 1)
            pool.affine_select(out=ident[:, :], in_=ident[:, :], compare_op=ALU.not_equal, fill=1.0, base=0,
                               pattern=[[-1, P]], channel_multiplier=1).then_inc(ident_ready, 1)
            pool.memset(kbd_hi[:, :, :].bitcast(F32), 0.0).then_inc(kbd_zero, 1)
            pool.memset(kbd_lo[:, :, :].bitcast(F32), 0.0).then_inc(kbd_zero, 1)

            def inverse_deviation(rows, unit):
                pool.wait_ge(aggregated, unit + 1)
                pool.tensor_tensor(var_eps[0:rows, :], mean_var[0:rows, :, 1], eps[0:rows, :], ALU.add).then_inc(var_done, 1)
                pool.wait_ge(var_done, unit + 1)
                pool.tensor_tensor(rstd[0:rows, :], var_eps[0:rows, :], minus_half[0:rows, :], ALU.pow).then_inc(rstd_done, 1)

            pool.memset(eps[:, :], EPS).then_inc(consts_ready, 1)
            pool.memset(minus_half[:, :], -0.5).then_inc(consts_ready, 1)
            pool.wait_ge(consts_ready, 2)
            inverse_deviation(NK, 0)
            for n, raw, hi, lo in (("v", raw_b, wv_hi, wv_lo), ("q", raw_a, wq_hi, wq_lo), ("o", raw_b, wo_hi, wo_lo)):
                pool.wait_ge(w_loaded[n], 16)
                pool.wait_ge(w_hi_done[n], 1)
                pool.tensor_tensor(lo[:, :, :], raw[:, :, :], hi[:, :, :].bitcast(F32), ALU.subtract).then_inc(w_lo_done[n], 1)
                if n == "v":
                    inverse_deviation(NK, 1)
                if n == "q":
                    inverse_deviation(P, 2)

            def batch(i):
                if is_at(i, TAIL):
                    return
                for s in range(SLOTS):
                    g, t = divmod(s, QT)
                    pool.wait_ge(inv_done, i * SLOTS + s + 1)
                    p = probs[:, g % 2, t, :].rearrange("p (h n) -> p h n", h=GH)
                    inv = row_inv[:, g % 2, t * GH:(t + 1) * GH].unsqueeze(2).broadcast_to([P, GH, NK])
                    last = pool.tensor_tensor(p, p, inv, ALU.mult)
                    last.then_inc(norm_done, 1)
                    if s == LN_SLOT + QT and not is_at(i, LAST):
                        inverse_deviation(P, i + CHUNKS + 1)
                    k = s - LNT_SLOT - 1
                    if 0 <= k < KT and not is_at(i, LAST):
                        pool.wait_ge(xhi_done, (i + CHUNKS + 1) * KT + k + 1)
                        pool.tensor_tensor(xn_lo[:, k, :], x_f[:, k % 2, :], xn_hi[:, k, :].bitcast(F32), ALU.subtract).then_inc(xn_ready, 1)

            each_batch(pool, batch)
            pool.wait_ge(norm_done, B * SLOTS)
            pool.sem_inc(attn_done, 1)


        @block.tensor
        def _(pe):
            def product(out, hi, lo, moving_hi, moving_lo, start, stop):
                pe.matmul(out, hi, moving_hi, start=start, stop=False)
                pe.matmul(out, lo, moving_hi, start=False, stop=False)
                return pe.matmul(out, hi, moving_lo, start=False, stop=stop)

            def transposes(src, rows, unit, k):
                if is_at(k, 0) or k == 0:
                    pe.wait_ge(ln_done, unit + 1)
                if not (is_at(unit, 0) and k == 0):
                    pe.wait_ge(xf_done, unit * KT + k)
                for t in range(QT):
                    mm = pe.transpose(ln_bank[:, t * rows:(t + 1) * rows], src[:, t, k * P:(k + 1) * P], ident[0:rows, 0:rows])
                mm.then_inc(lnt_ready, 1)

            def q_unit(m, k):
                return product(proj[m % 2][:, :], wq_hi[:, k, m * P:(m + 1) * P], wq_lo[:, k, m * P:(m + 1) * P],
                               xn_hi[:, k, :], xn_lo[:, k, :], k == 0, k == KT - 1)

            pe.wait_ge(ident_ready, 1)
            for k in range(KT):
                transposes(ctx_tok[0], NK, 0, k)
            for c in range(CHUNKS):
                hi, lo = cn[c]
                following = (ctx_tok[1], NK) if c == 0 else (x_tok, P)
                if c == 0:
                    pe.wait_ge(w_lo_done["k"], 1)
                pe.wait_ge(xn_ready, (c + 1) * KT)
                for g in range(NG):
                    if c > 0 and g < 2:
                        pe.wait_ge(v_evac, (c - 1) * CB + 3 + g)
                    elif g >= 2:
                        pe.wait_ge(k_evac, c * NG + g - 1)
                    for k in range(KT):
                        mm = product(proj[g % 2][:, 0:CTOK], wk_hi[:, k, g * P:(g + 1) * P], wk_lo[:, k, g * P:(g + 1) * P],
                                     hi[:, k, 0:CTOK], lo[:, k, 0:CTOK], k == 0, k == KT - 1)
                    mm.then_inc(k_mm, 1)
                    transposes(*following, c + 1, g)
                if c == 0:
                    pe.wait_ge(w_lo_done["v"], 1)
                for b in range(CB):
                    if b < 2:
                        pe.wait_ge(k_evac, c * NG + 3 + b)
                    else:
                        pe.wait_ge(v_evac, c * CB + b - 1)
                    for k in range(KT):
                        tok = slice(b * NK, (b + 1) * NK)
                        mm = product(proj[b % 2][0:NK, :], hi[:, k, tok], lo[:, k, tok],
                                     wv_hi[:, k, :], wv_lo[:, k, :], k == 0, k == KT - 1)
                    mm.then_inc(v_mm, 1)

            pe.wait_ge(w_lo_done["q"], 1)
            pe.wait_ge(xn_ready, (CHUNKS + 1) * KT)
            pe.wait_ge(v_evac, CHUNKS * CB - 1)
            for k in range(KT):
                mm = q_unit(0, k)
            mm.then_inc(q_mm, 1)

            def batch(i):
                first, last, tail = is_at(i, FIRST), is_at(i, LAST), is_at(i, TAIL)

                def q_units(todo, of):
                    for m, k in todo:
                        if k == 0:
                            if m == 3:
                                pe.wait_ge(q_ready, of * NG + 2)
                            elif m > 0:
                                pe.wait_ge(q_ready, of * NG + 1)
                                if first and m == 1:
                                    pe.wait_ge(v_evac, CHUNKS * CB)
                            else:
                                if first:
                                    pe.wait_ge(q_ready, 3)
                                else:
                                    pe.wait_ge(x2_evac, (of - 2) * KT + 3)
                                pe.wait_ge(xn_ready, (of + CHUNKS + 1) * KT)
                        mm = q_unit(m, k)
                        if k == KT - 1:
                            mm.then_inc(q_mm, 1)

                for s in range(SLOTS):
                    g, t = divmod(s, QT)
                    n = i * SLOTS + s
                    if not tail:
                        if t == 0:
                            pe.wait_ge(q_ready, i * NG + g + 1)
                            if g % 2 == 0:
                                pe.wait_ge(kbd_loaded[g // 2], (i + 1) * 2 * GH * 16)
                        if not (first and s < 2):
                            pe.wait_ge(exp_done, n - 1)
                        rows = slice(t * P, (t + 1) * P)
                        product(s_bank[s % 2][:, 0:GH * NK], q_hi[:, g, rows], q_lo[:, g, rows],
                                kbd_hi[:, g, :], kbd_lo[:, g, :], True, True).then_inc(s_ready, 1)
                    if not (first and s < T_LAG) and not (tail and s >= T_LAG):
                        h = (s - T_LAG) % GH
                        gg = ((s - T_LAG) % SLOTS) // GH
                        if h == 0:
                            pe.wait_ge(norm_done, n - T_LAG + GH)
                        if not (first and s < T_LAG + 2):
                            pe.wait_ge(pt_ready, n - T_LAG - 1)
                        for tt in range(QT):
                            mm = pe.transpose(t_bank[s % 2][0:NK, tt * P:(tt + 1) * P],
                                              probs[:, gg % 2, tt, h * NK:(h + 1) * NK], ident[:, :])
                        mm.then_inc(t_ready, 1)
                    if not tail:
                        q_units(units(Q_NOW, s, 1), i)
                    for m, k in units(WO_BEFORE, s) if not first else ():
                        if m == 0:
                            pe.wait_ge(o_ready, (i - 1) * NG + k + 1)
                        if k == 0:
                            if m >= 2:
                                pe.wait_ge(x2_evac, (i - 1) * KT + m - 1)
                            elif tail:
                                pe.wait_ge(x2_evac, (i - 2) * KT + 3 + m)
                            else:
                                pe.wait_ge(q_ready, i * NG + 3 + m)
                        mm = product(proj[m % 2][:, :], wo_hi[:, k, m * P:(m + 1) * P], wo_lo[:, k, m * P:(m + 1) * P],
                                     o_hi[:, k, :], o_lo[:, k, :], k == 0, k == KT - 1)
                        if k == KT - 1:
                            mm.then_inc(wo_mm, 1)
                    if not tail and not last:
                        q_units(units(Q_NEXT, s), i + 1)
                    if not tail and not last and LNT_SLOT <= s < LNT_SLOT + KT:
                        transposes(x_tok, P, i + CHUNKS + 1, s - LNT_SLOT)
                    if s % 4 == PV_LAG % 4 and not (first and s < PV_LAG) and not (tail and s >= PV_LAG):
                        gg = ((s - PV_LAG) % SLOTS) // GH
                        done = i * NG + (s - PV_LAG) // GH
                        pe.wait_ge(pt_ready, done * GH + GH)
                        if gg == 0:
                            pe.wait_ge(v_loaded, 16 * (i + 1))
                        if not (first and s == PV_LAG):
                            pe.wait_ge(o_ready, done)
                        for h in range(GH):
                            head = gg * GH + h
                            mm = pe.matmul(o_bank[h * HD:(h + 1) * HD, :], v_now[0:NK, head * HD:(head + 1) * HD],
                                           probs_t[0:NK, (gg % 2) * GH + h, :], start=True, stop=True)
                        mm.then_inc(o_mm, 1)

            pe.wait_ge(w_lo_done["o"], 1)
            each_batch(pe, batch)

            def ffn(b):
                first = is_at(b, 0)
                for m in range(FT + 1):
                    if m < FT:
                        if first:
                            pe.wait_ge(wlo2_done, m + 1)
                        if not (first and m < 4):
                            pe.wait_ge(silu_done, b * FT + m - 3)
                        for k in range(KT):
                            if m == 0:
                                pe.wait_ge(x2_split, b * KT + k + 1)
                            mm = product(acc1[m % 4][:, :], w1_hi[:, m, k * P:(k + 1) * P], w1_lo[:, m, k * P:(k + 1) * P],
                                         x2_hi[:, k, :], x2_lo[:, k, :], k == 0, k == KT - 1)
                        mm.then_inc(f1_mm, 1)
                    if m > 0:
                        f = m - 1
                        pe.wait_ge(h_ready, b * FT + f + 1)
                        for o in range(KT):
                            if f == 0 and not first:
                                pe.wait_ge(y_done, (b - 1) * KT + o + 1)
                            mm = product(acc2[o][:, :], w2_hi[:, f, o * P:(o + 1) * P], w2_lo[:, f, o * P:(o + 1) * P],
                                         h_hi[:, f % 2, :], h_lo[:, f % 2, :], f == 0, f == FT - 1)
                            if f == FT - 1:
                                mm.then_inc(f2_mm, 1)

            ffn(0)
            with pe.Fori(1, B) as b:
                ffn(b)

        @block.scalar
        def _(act):
            for n, raw, hi in (("k", raw_a, wk_hi), ("v", raw_b, wv_hi), ("q", raw_a, wq_hi), ("o", raw_b, wo_hi)):
                def split(n=n, raw=raw, hi=hi):
                    act.wait_ge(w_loaded[n], 16)
                    act.activation(hi[:, :, :], raw[:, :, :], ACT.Copy).then_inc(w_hi_done[n], 1)
                if n in "kv":
                    split()
                if n == "q":
                    split()
                if n == "o":
                    split_o = split
            for c in range(CHUNKS):
                for g in range(NG):
                    act.wait_ge(k_mm, c * NG + g + 1)
                    if c * NG + g >= 2:
                        act.wait_ge(k_stored[g % 2], 32 * ((c * NG + g) // 2))
                    act.activation(k_out_hi[:, g % 2, :], proj[g % 2][:, 0:CTOK], ACT.Copy).then_inc(khi_done, 1)
                if c == 0:
                    split_o()
                for b in range(CB):
                    act.wait_ge(v_mm, c * CB + b + 1)
                    if c * CB + b >= 2:
                        act.wait_ge(stored[b % 2], 16 * ((c * CB + b) // 2))
                    act.activation(v_out[0:NK, b % 2, :], proj[b % 2][0:NK, :], ACT.Copy).then_inc(v_evac, 1)

            def q_out(m, of):
                act.wait_ge(q_mm, of * NG + m + 1)
                act.activation(q_hi[:, m, :], proj[m % 2][:, :], ACT.Copy, scale=SCALE).then_inc(qhi_done, 1)

            q_out(0, 0)
            act.wait_ge(w_lo_done["o"], 1)

            def batch(i):
                first, last, tail = is_at(i, FIRST), is_at(i, LAST), is_at(i, TAIL)
                for s in range(SLOTS):
                    g, t = divmod(s, QT)
                    n = i * SLOTS + s
                    if s in Q_EVAC and not tail:
                        if Q_EVAC[s] > 0:
                            q_out(Q_EVAC[s], i)
                        elif not last:
                            q_out(0, i + 1)
                    if not tail:
                        act.wait_ge(max_done, n + 1)
                        if t == 0 and not (first and g < 2):
                            act.wait_ge(t_ready, n - 4)
                        for h in range(GH):
                            c = t * GH + h
                            e = act.activation(probs[:, g % 2, t, h * NK:(h + 1) * NK], s_bank[s % 2][:, h * NK:(h + 1) * NK], ACT.Exp,
                                               bias=neg_max[:, g % 2, c:c + 1], accum_out=row_sum[:, g % 2, c:c + 1])
                        e.then_inc(exp_done, 1)
                    if not (first and s < T_LAG) and not (tail and s >= T_LAG):
                        h = (s - T_LAG) % GH
                        gg = ((s - T_LAG) % SLOTS) // GH
                        act.wait_ge(t_ready, n - T_LAG + 1)
                        if h == 0 and not (first and gg < 2):
                            act.wait_ge(o_mm, i * NG + (s - T_LAG) // GH - 1)
                        act.activation(probs_t[0:NK, (gg % 2) * GH + h, :], t_bank[s % 2][0:NK, :], ACT.Copy).then_inc(pt_ready, 1)
                    if s in OUT_STEP and not (first and OUT_STEP[s] > 1) and not (tail and OUT_STEP[s] < 2):
                        gg = OUT_STEP[s]
                        act.wait_ge(o_mm, i * NG + gg + 1 - (NG if gg > 1 else 0))
                        if gg == 0 and not first:
                            act.wait_ge(wo_mm, i * KT)
                        act.activation(o_hi[:, gg, :], o_bank[:, :], ACT.Copy).then_inc(ohi_done, 1)

            each_batch(act, batch)
            act.wait_ge(ohi_done, B * NG)
            act.sem_inc(attn_done, 1)

            def split2(m):
                if m == 0:
                    act.wait_ge(attn_done, 4)
                act.wait_ge(wraw_loaded[m % 2], 32 * (m // 2 + 1))
                act.activation(w1_hi[:, m, :], w_raw[:, m % 2, 0, :], ACT.Copy)
                act.activation(w2_hi[:, m, :], w_raw[:, m % 2, 1, :], ACT.Copy).then_inc(whi2_done, 1)

            def hidden(b, m):
                act.wait_ge(f1_mm, b * FT + m + 1)
                if not (is_at(b, 0) and m < 2):
                    act.wait_ge(h_ready, b * FT + m - 1)
                act.activation(h_f[:, m % 2, :], acc1[m % 4][:, :], ACT.Silu, bias=vec[:, V_B1 + m:V_B1 + m + 1]).then_inc(silu_done, 1)

            split2(0)
            split2(1)
            for m in range(FT):
                hidden(0, m)
                if m + 2 < FT:
                    split2(m + 2)
            with act.Fori(1, B) as b:
                for m in range(FT):
                    hidden(b, m)

        @block.vector
        def _(dve):
            def ln_stats(src, rows, t):
                dve.bn_stats(stats[0:rows, t, :], src[:, t, :]).then_inc(stats_step, 1)

            def ln_aggregate(rows):
                for t in range(QT):
                    ins = dve.bn_aggr(mean_var[0:rows, t, :], stats[0:rows, t, :])
                ins.then_inc(aggregated, 1)

            def ln_apply(src, rows, unit):
                dve.wait_ge(rstd_done, unit + 1)
                for t in range(QT):
                    ins = dve.tensor_scalar(src[:, t, :], src[:, t, :], mean_var[0:rows, t, 0:1], rstd[0:rows, t:t + 1],
                                            ALU.subtract, ALU.mult)
                ins.then_inc(ln_done, 1)

            def ln_out(unit, k, width, hi, lo, v_g, v_b):
                if not isinstance(unit, int) or unit > 0:
                    dve.wait_ge(xn_ready, unit * KT + k - 1)
                dve.wait_ge(lnt_ready, unit * KT + k + 1)
                dve.tensor_scalar(x_f[:, k % 2, 0:width], ln_bank[:, 0:width], vec[:, v_g + k:v_g + k + 1], vec[:, v_b + k:v_b + k + 1],
                                  ALU.mult, ALU.add).then_inc(xf_done, 1)
                dve.wait_ge(xf_done, unit * KT + k + 1)
                dve.tensor_copy(hi[:, k, 0:width], x_f[:, k % 2, 0:width]).then_inc(xhi_done, 1)
                if isinstance(unit, int) and unit <= CHUNKS:
                    dve.wait_ge(xhi_done, unit * KT + k + 1)
                    dve.tensor_tensor(lo[:, k, 0:width], x_f[:, k % 2, 0:width], hi[:, k, 0:width].bitcast(F32), ALU.subtract).then_inc(xn_ready, 1)

            def q_low(m, of):
                dve.wait_ge(qhi_done, of * NG + m + 1)
                dve.scalar_tensor_tensor(q_lo[:, m, :], proj[m % 2][:, :], SCALE, q_hi[:, m, :].bitcast(F32),
                                         ALU.mult, ALU.subtract).then_inc(q_ready, 1)

            dve.wait_ge(ctx_loaded[0], 16)
            for t in range(QT):
                ln_stats(ctx_tok[0], NK, t)
            dve.wait_ge(stats_step, QT)
            ln_aggregate(NK)
            ln_apply(ctx_tok[0], NK, 0)
            dve.wait_ge(w_hi_done["k"], 1)
            dve.tensor_tensor(wk_lo[:, :, :], raw_a[:, :, :], wk_hi[:, :, :].bitcast(F32), ALU.subtract).then_inc(w_lo_done["k"], 1)
            dve.wait_ge(vec_loaded, 16)
            for k in range(KT):
                ln_out(0, k, CTOK, *cn[0], V_GK, V_BK)
            dve.wait_ge(ctx_loaded[1], 16)
            for t in range(QT):
                ln_stats(ctx_tok[1], NK, t)
            dve.wait_ge(stats_step, 2 * QT)
            ln_aggregate(NK)
            ln_apply(ctx_tok[1], NK, 1)
            for c in range(CHUNKS):
                if c == 1:
                    dve.wait_ge(x_loaded, 16)
                for g in range(NG):
                    dve.wait_ge(khi_done, c * NG + g + 1)
                    dve.tensor_tensor(k_out_lo[:, g % 2, :], proj[g % 2][:, 0:CTOK], k_out_hi[:, g % 2, :].bitcast(F32),
                                      ALU.subtract).then_inc(k_evac, 1)
                    if c == 0:
                        ln_out(1, g, CTOK, *cn[1], V_GK, V_BK)
                    else:
                        ln_out(2, g, NQ, xn_hi, xn_lo, V_GQ, V_BQ)
                if c == 0:
                    dve.wait_ge(x_loaded, 16)
                    for t in range(QT):
                        ln_stats(x_tok, P, t)
                    dve.wait_ge(stats_step, 3 * QT)
                    ln_aggregate(P)
                    ln_apply(x_tok, P, 2)
            q_low(0, 0)

            def inverse(n, g, t):
                dve.wait_ge(exp_done, n + 1)
                c = slice(t * GH, (t + 1) * GH)
                dve.reciprocal(row_inv[:, g % 2, c], row_sum[:, g % 2, c]).then_inc(inv_done, 1)

            def batch(i):
                first, last, tail = is_at(i, FIRST), is_at(i, LAST), is_at(i, TAIL)
                for s in range(SLOTS):
                    g, t = divmod(s, QT)
                    n = i * SLOTS + s
                    aggregate = not tail and not last and s == LN_SLOT + QT
                    if aggregate:
                        dve.wait_ge(stats_step, (i + CHUNKS + 2) * QT)
                    if not tail:
                        dve.wait_ge(s_ready, n + 1)
                        c = slice(t * GH, (t + 1) * GH)
                        dve.tensor_reduce(neg_max[:, g % 2, c], s_bank[s % 2][:, 0:GH * NK].rearrange("p (h n) -> p h n", h=GH),
                                          AX.X, ALU.max, negate=True).then_inc(max_done, 1)
                    if aggregate:
                        ln_aggregate(P)
                    if not (first and s == 0) and not (tail and s > 0):
                        pg, pt = divmod((s - 1) % SLOTS, QT)
                        inverse(n - 1, pg, pt)
                    if s in Q_EVAC and not tail:
                        if Q_EVAC[s] > 0:
                            q_low(Q_EVAC[s], i)
                        elif not last:
                            q_low(0, i + 1)
                    if not tail and not last:
                        if LN_SLOT <= s < LN_SLOT + QT:
                            if s == LN_SLOT:
                                dve.wait_ge(x_loaded, 16 * (i + 2))
                            ln_stats(x_tok, P, s - LN_SLOT)
                        if s == LN_APPLY:
                            ln_apply(x_tok, P, i + CHUNKS + 1)
                        if LNT_SLOT + 1 <= s < LNT_SLOT + 1 + KT:
                            ln_out(i + CHUNKS + 1, s - LNT_SLOT - 1, NQ, xn_hi, xn_lo, V_GQ, V_BQ)
                    if not first and s in X2_EVAC:
                        m = X2_EVAC[s]
                        dve.wait_ge(wo_mm, (i - 1) * KT + m + 1)
                        if m == 0:
                            dve.wait_ge(xT_loaded, 16 * i)
                        dve.wait_ge(stored[m % 2], V_STORES + 16 * KT // 2 * (i - 1) + 16 * (m // 2))
                        dve.scalar_tensor_tensor(x2_out[:, m % 2, :], proj[m % 2][:, :], vec[:, V_BO + m:V_BO + m + 1], xT_now[:, m, :],
                                                 ALU.add, ALU.add).then_inc(x2_evac, 1)
                    if s in OUT_STEP and not (first and OUT_STEP[s] > 1) and not (tail and OUT_STEP[s] < 2):
                        gg = OUT_STEP[s]
                        dve.wait_ge(ohi_done, i * NG + gg + 1 - (NG if gg > 1 else 0))
                        dve.tensor_tensor(o_lo[:, gg, :], o_bank[:, :], o_hi[:, gg, :].bitcast(F32), ALU.subtract).then_inc(o_ready, 1)

            each_batch(dve, batch)
            dve.wait_ge(x2_evac, B * KT)
            dve.sem_inc(attn_done, 2)

            def split2(m):
                dve.wait_ge(whi2_done, m + 1)
                dve.tensor_tensor(w1_lo[:, m, :], w_raw[:, m % 2, 0, :], w1_hi[:, m, :].bitcast(F32), ALU.subtract)
                dve.tensor_tensor(w2_lo[:, m, :], w_raw[:, m % 2, 1, :], w2_hi[:, m, :].bitcast(F32), ALU.subtract).then_inc(wlo2_done, 1)

            def split_x2(b):
                dve.wait_ge(x2_loaded, 16 * (b + 1))
                if not is_at(b, 0):
                    dve.wait_ge(f1_mm, b * FT)
                for k in range(KT):
                    dve.tensor_copy(x2_hi[:, k, :], x2_in[:, k, :]).then_inc(x2hi_done, 1)
                for k in range(KT):
                    dve.wait_ge(x2hi_done, b * KT + k + 1)
                    dve.tensor_tensor(x2_lo[:, k, :], x2_in[:, k, :], x2_hi[:, k, :].bitcast(F32), ALU.subtract).then_inc(x2_split, 1)

            def hidden(b, m):
                dve.wait_ge(silu_done, b * FT + m + 1)
                dve.tensor_copy(h_hi[:, m % 2, :], h_f[:, m % 2, :]).then_inc(hhi_done, 1)
                dve.wait_ge(hhi_done, b * FT + m + 1)
                dve.tensor_tensor(h_lo[:, m % 2, :], h_f[:, m % 2, :], h_hi[:, m % 2, :].bitcast(F32), ALU.subtract).then_inc(h_ready, 1)

            def finish(b):
                dve.wait_ge(res_ready, 16 * (b + 1))
                for o in range(KT):
                    dve.wait_ge(f2_mm, b * KT + o + 1)
                    dve.wait_ge(stored[o % 2], X2_STORES + 16 * KT // 2 * b + 16 * (o // 2))
                    dve.scalar_tensor_tensor(y_out[:, o % 2, :], acc2[o][:, :], vec[:, V_B2 + o:V_B2 + o + 1], x2_res[:, o, :],
                                             ALU.add, ALU.add).then_inc(y_done, 1)

            dve.wait_ge(attn_done, 4)
            split_x2(0)
            split2(0)
            split2(1)
            for m in range(FT):
                hidden(0, m)
                if m + 2 < FT:
                    split2(m + 2)
            with dve.Fori(1, B) as b:
                split_x2(b)
                finish(b - 1)
                for m in range(FT):
                    hidden(b, m)
            finish(B - 1)


def kernel(**inputs):
    import numpy as np
    import concourse.bacc as bacc
    from concourse.bass_utils import run_bass_kernel_spmd as run

    a = {k.removeprefix("L0_xattn_"): np.asarray(v) for k, v in inputs.items()}

    def cols(v):
        return v.reshape(-1, P).T

    c = np.ascontiguousarray
    wkv = a["Wkv"]
    arrays = {
        "in_x": c(a["x"]),
        "in_xT": c(a["x"].reshape(B, NQ, KT, P).transpose(0, 3, 2, 1)),
        "in_ctx": c(a["ctx_1024"].reshape(B * NK, D)),
        "in_wqT": c(a["Wq"].T),
        "in_wkT": c(wkv[0:D].T),
        "in_wvT": c(wkv[D:2 * D].T),
        "in_woT": c(a["Wo"].T),
        "in_w1": c(a["W1"].reshape(FT, P, KT, P).transpose(0, 3, 2, 1).reshape(FT, P, KT * P)),
        "in_w2": c(a["W2"].T.reshape(FT, P, D)),
        "in_vecs": c(np.concatenate([cols(a[n]) for n in ("ln_q_g", "ln_q_b", "ln_kv_g", "ln_kv_b", "bo", "b2", "b1")], axis=1)),
    }
    nc = bacc.Bacc("TRN2", target_bir_lowering=False, num_devices=1)
    args = [nc.dram_tensor(n, v.shape, mybir.dt.from_np(v.dtype), kind="ExternalInput").ap() for n, v in arrays.items()]
    args.append(nc.dram_tensor("out_y", (B, KT, P, NQ), F32, kind="ExternalOutput").ap())
    cross_attention_block(nc, *args)
    y = run(nc, [arrays], core_ids=[0]).results[0]["out_y"]
    return y.transpose(0, 3, 1, 2).reshape(B, NQ, D)
```

```python
from contextlib import ExitStack

import concourse.bass as bass
from concourse import mybir

F32 = mybir.dt.float32
F32R = mybir.dt.float32r
ALU = mybir.AluOpType
ACT = mybir.ActivationFunctionType
AX = mybir.AxisListType

P = 128
B, NQ, D = 8, 512, 512
NK = 120
H, HD = 16, 32
DFF = 4 * D
KT = D // P
GH = P // HD
NG = H // GH
QT = NQ // P
FT = DFF // P
CB = 4
CHUNKS = B // CB
CTOK = CB * NK
SCALE = float(HD) ** -0.5
EPS = 1e-5
V_GQ, V_BQ, V_GK, V_BK, V_BO, V_B2, V_B1 = 0, KT, 2 * KT, 3 * KT, 4 * KT, 5 * KT, 6 * KT
NV = 6 * KT + FT

SLOTS = NG * QT
T_LAG = 5
PV_STEP = {9: 0, 14: 1, 1: 2, 5: 3}
OUT_STEP = {13: 0, 15: 1, 2: 2, 6: 3}
LN_SLOT = 0
LN_APPLY = 6
LNT_SLOT = 7
Q_NEXT = {13: 2, 14: 2, 15: 2}
Q_NOW = {0: 2, 1: 2, 2: 2, 3: 2, 4: 2}
WO_BEFORE = {5: 2, 6: 1, 7: 2, 8: 2, 9: 2, 10: 2, 11: 2, 12: 3}
Q_EVAC = {1: 1, 3: 2, 5: 3, 15: 0}
X2_EVAC = {8: 0, 10: 1, 12: 2, 13: 3}

X2_SPLIT = {8: 0, 9: 1, 10: 2, 11: 3}
LAST_W_HI, LAST_W_LO = {8: 0, 10: 1}, {12: 0, 14: 1}
TAIL_HIDDEN = {1: 0, 3: 1}
TAIL_SILU = {4: 0, 6: 1}
TAIL_H = {5: 0, 7: 1}
TAIL_W_HI, TAIL_W_LO = {5: 2, 8: 3}, {6: 2, 8: 3}


def units(table, step, skip=0):
    done = skip + sum(n for s, n in table.items() if s < step)
    return [divmod(done + j, KT) for j in range(table.get(step, 0))]


def cross_attention_block(nc, x, xT, ctx_in, wqT, wkT, wvT, woT, w1c, w2c, vecs, yT):
    k_scr = nc.dram_tensor("k_scratch", [B, P, NG, 2, NK], F32).ap()
    v_scr = nc.dram_tensor("v_scratch", [B, P, D], F32).ap()
    x2_scr = nc.dram_tensor("x2_scratch", [B, KT, P, NQ], F32).ap()

    with ExitStack() as outer:
        def sem(name):
            return outer.enter_context(nc.semaphore(name))

        vec = outer.enter_context(nc.sbuf_tensor("vec", [P, NV], F32))
        bank = [outer.enter_context(nc.psum_tensor(f"bank{i}", [P, 512], F32)) for i in range(8)]

        def placed(place, name, shape, dt=F32):
            return place.enter_context(nc.sbuf_tensor(name, shape, dt))

        def weights(m, place):
            return [placed(place, f"{n}_{m}", [P, 512], F32R) for n in ("w1_hi", "w1_lo", "w2_hi", "w2_lo")]

        ffn_w = [weights(0, outer)]

        early = ExitStack()

        def sb(name, shape, dt=F32):
            return early.enter_context(nc.sbuf_tensor(name, shape, dt))

        wk_hi, wk_lo = sb("wk_hi", [P, KT, D], F32R), sb("wk_lo", [P, KT, D], F32R)
        wv_hi, wv_lo = sb("wv_hi", [P, KT, D], F32R), sb("wv_lo", [P, KT, D], F32R)
        wq_hi, wq_lo = sb("wq_hi", [P, KT, D], F32R), sb("wq_lo", [P, KT, D], F32R)
        x_tok = sb("x_tok", [P, QT, D])
        xn = sb("xn", [P, 2, KT, NQ], F32R)
        xn_hi, xn_lo = xn[:, 0, :, :], xn[:, 1, :, :]
        q_hi, q_lo = sb("q_hi", [P, KT, NQ], F32R), sb("q_lo", [P, KT, NQ], F32R)
        k_diag = sb("k_diag", [P, NG, 2, GH * NK], F32R)
        wo_hi, wo_lo = sb("wo_hi", [P, KT, D], F32R), sb("wo_lo", [P, KT, D], F32R)
        ident = sb("ident", [P, P])
        stats = sb("stats", [P, QT, 6])
        mean_var = sb("mean_var", [P, QT, 2])
        eps, var_eps, minus_half, rstd = (sb(n, [P, QT]) for n in ("eps", "var_eps", "minus_half", "rstd"))
        x_f = sb("x_f", [P, 2, NQ])
        o_hi, o_lo = sb("o_hi", [P, KT, NQ], F32R), sb("o_lo", [P, KT, NQ], F32R)
        v_now = sb("v_now", [P, D])
        probs = sb("probs", [P, 2, QT, GH * NK])
        probs_t = sb("probs_t", [P, 2 * GH, NQ])
        neg_max = sb("neg_max", [P, 2, QT * GH])
        row_sum = sb("row_sum", [P, 2, QT * GH])
        row_inv = sb("row_inv", [P, 2, QT * GH])
        xT_now = sb("xT_now", [P, KT, NQ])
        x2_out = sb("x2_out", [P, 2, NQ])
        early.close()

        late = ExitStack()
        outer.enter_context(late)

        def sl(name, shape, dt=F32):
            return late.enter_context(nc.sbuf_tensor(name, shape, dt))

        w_raw = sl("w_raw", [P, 2, 2, 512])
        x2_in = sl("x2_in", [P, KT, NQ])
        x2_hi, x2_lo = sl("x2_hi", [P, KT, NQ], F32R), sl("x2_lo", [P, KT, NQ], F32R)
        ffn_w += [weights(m, late) for m in range(1, 4)]
        h_f = sl("h_f", [P, 2, NQ])
        h_hi, h_lo = sl("h_hi", [P, 2, NQ], F32R), sl("h_lo", [P, 2, NQ], F32R)
        Q_OVER = 7
        ffn_w += [weights(m, late) for m in range(4, Q_OVER)]
        x2_res = sl("x2_res", [P, KT, NQ])
        ffn_w += [weights(m, late) for m in range(Q_OVER, FT)]

        y_out = w_raw[:, :, :, :].rearrange("p a b n -> p (a b) n")

        raw_a = xT_now
        raw_b = probs[:, :, :, :].rearrange("p a t n -> p (a t n)")[:, 0:KT * D].rearrange("p (k n) -> p k n", k=KT)
        ctx_tok = [probs_t[0:NK, c * CB:(c + 1) * CB, :] for c in range(CHUNKS)]
        cn = [(q_hi, q_lo), (o_hi, o_lo)]
        k_out = [place[:, 0:CB * NG * 2 * NK].rearrange("p (b g t n) -> p b g t n", b=CB, g=NG, t=2)
                 for place in (xn[:, :, :, :].rearrange("p a k n -> p (a k n)"),
                               probs_t[:, :, :].rearrange("p h n -> p (h n)").bitcast(F32R))]
        v_out = x2_out

        k_bank, v_bank = [bank[1], bank[2], bank[3], bank[4]], bank[5:7]
        ln_bank, proj, s_bank, t_bank, o_bank = bank[0], bank[1:3], bank[3:5], bank[5:7], bank[7]
        acc2 = [bank[0], bank[7], bank[1], bank[2]]
        acc1 = bank[3:7]

        vec_loaded, ident_zero, ident_ready, consts_ready, k_zero = sem("vec_loaded"), sem("ident_zero"), sem("ident_ready"), sem("consts_ready"), sem("k_zero")
        ctx0_loaded, ctx1_loaded = [sem(f"ctx0_loaded{t}") for t in range(CB)], sem("ctx1_loaded")
        x_loaded, xT_loaded, v_loaded = sem("x_loaded"), sem("xT_loaded"), sem("v_loaded")
        k_loaded = [sem("k01_loaded"), sem("k23_loaded")]
        w_loaded = {n: sem(f"w{n}_loaded") for n in "kvqo"}
        w_hi_done = {n: sem(f"w{n}_hi_done") for n in "kvqo"}
        w_lo_done = {n: sem(f"w{n}_lo_done") for n in "kvqo"}
        k_stored = [sem(f"k_stored{c}") for c in range(CHUNKS)]
        K_STORES = 16
        stored = [sem("stored0"), sem("stored1")]
        V_STORES = 16 * B // 2
        X2_STORES = V_STORES + 16 * B * KT // 2
        Y_STORES = X2_STORES + 16 * B * KT // 2
        stats_step, aggregated, var_done, rstd_done, ln_done = sem("stats_step"), sem("aggregated"), sem("var_done"), sem("rstd_done"), sem("ln_done")
        lnt_ready, xf_done, xhi_done, xn_ready = sem("lnt_ready"), sem("xf_done"), sem("xhi_done"), sem("xn_ready")
        k_mm, v_mm, q_mm, wo_mm = sem("k_mm"), sem("v_mm"), sem("q_mm"), sem("wo_mm")
        khi_done, k_evac, v_evac = sem("khi_done"), sem("k_evac"), sem("v_evac")
        qhi_done, q_ready, x2_evac = sem("qhi_done"), sem("q_ready"), sem("x2_evac")
        s_ready, max_done, exp_done, inv_done, norm_done = (sem(n) for n in ("s_ready", "max_done", "exp_done", "inv_done", "norm_done"))
        t_ready, pt_ready, o_mm, ohi_done, o_ready = (sem(n) for n in ("t_ready", "pt_ready", "o_mm", "ohi_done", "o_ready"))
        attn_done = sem("attn_done")
        wraw_loaded, whi2_done, wlo2_done = [sem("wraw_loaded0"), sem("wraw_loaded1")], sem("whi2_done"), sem("wlo2_done")
        x2_loaded, x2hi_done, x2_split, res_ready = sem("x2_loaded"), sem("x2hi_done"), sem("x2_split"), sem("res_ready")
        f1_mm, silu_done, hhi_done, h_ready, f2_mm, y_done = (sem(n) for n in ("f1_mm", "silu_done", "hhi_done", "h_ready", "f2_mm", "y_done"))

        FIRST, LAST, TAIL = 0, B - 1, B

        def is_at(i, n):
            return isinstance(i, int) and i == n

        def each_batch(eng, step):
            step(FIRST)
            with eng.Fori(1, LAST) as i:
                step(i)
            step(LAST)
            step(TAIL)

        block = outer.enter_context(nc.Block())

        @block.sync
        def _(sp):
            for t in range(CB):
                sp.dma_start(ctx_tok[0][:, t, :], ctx_in[t * NK:(t + 1) * NK, :]).then_inc(ctx0_loaded[t], 16)
            sp.dma_start(raw_a[:, :, :], wkT.rearrange("(k p) n -> p k n", p=P)).then_inc(w_loaded["k"], 16)
            sp.dma_start(vec[:, :], vecs).then_inc(vec_loaded, 16)
            sp.dma_start(raw_b, wvT.rearrange("(k p) n -> p k n", p=P)).then_inc(w_loaded["v"], 16)
            sp.dma_start(ctx_tok[1], ctx_in[CTOK:2 * CTOK, :].rearrange("(t p) d -> p t d", p=NK)).then_inc(ctx1_loaded, 16)
            sp.dma_start(x_tok[:, :, :], x[0].rearrange("(t p) d -> p t d", p=P)).then_inc(x_loaded, 16)
            sp.wait_ge(w_lo_done["k"], KT)
            sp.dma_start(raw_a[:, :, :], wqT.rearrange("(k p) n -> p k n", p=P)).then_inc(w_loaded["q"], 16)
            sp.wait_ge(w_lo_done["v"], 1)
            sp.dma_start(raw_b, woT.rearrange("(k p) n -> p k n", p=P)).then_inc(w_loaded["o"], 16)
            def load_x(b):
                sp.wait_ge(lnt_ready, (b + CHUNKS) * KT)
                sp.dma_start(x_tok[:, :, :], x[b].rearrange("(t p) d -> p t d", p=P)).then_inc(x_loaded, 16)

            def load_k(b, half):
                groups = slice(2 * half, 2 * half + 2)
                for j in range(GH):
                    rows = slice(HD * j, HD * (j + 1))
                    sp.dma_start(k_diag[rows, groups, :, j * NK:(j + 1) * NK].bitcast(F32),
                                 k_scr[b, rows, groups, :, :]).then_inc(k_loaded[half], 16)

            def store_v(b):
                sp.wait_ge(v_evac, b + 1)
                sp.dma_start(v_scr[b, 0:NK], v_out[0:NK, b % 2, :]).then_inc(stored[b % 2], 16)

            for c in range(CHUNKS):
                if c == 1:
                    load_x(1)
                sp.wait_ge(k_evac, (c + 1) * NG)
                sp.dma_start(k_scr[c * CB:(c + 1) * CB].rearrange("b p g t n -> p b (g t n)"),
                             k_out[c].bitcast(F32).rearrange("p b g t n -> p b (g t n)")).then_inc(k_stored[c], 16)
                if c == 0:
                    for b in range(CB):
                        store_v(b)
                    sp.wait_ge(k_stored[0], K_STORES)
                    sp.wait_ge(k_zero, 1)
                    load_k(0, 0)
                    load_k(0, 1)
            sp.wait_ge(k_stored[1], K_STORES)
            for s in range(2):
                sp.wait_ge(stored[s], V_STORES // CHUNKS)

            def load_weights(m):
                if m >= 2:
                    sp.wait_ge(wlo2_done, m - 1)
                sp.dma_start(w_raw[:, m % 2, 0, :], w1c[m]).then_inc(wraw_loaded[m % 2], 16)
                sp.dma_start(w_raw[:, m % 2, 1, :], w2c[m]).then_inc(wraw_loaded[m % 2], 16)

            def batch(i):
                first, tail = is_at(i, FIRST), is_at(i, TAIL)
                if is_at(i, LAST):
                    for s in range(2):
                        sp.wait_ge(stored[s], V_STORES + 16 * KT // 2)
                    sp.dma_start(x2_in[:, :, :], x2_scr[0].rearrange("k p n -> p k n")).then_inc(x2_loaded, 16)
                    load_weights(0)
                    load_weights(1)
                if not first and not tail and not is_at(i, LAST):
                    load_x(i + 1)
                if not first:
                    if not tail:
                        sp.wait_ge(s_ready, i * SLOTS)
                        load_k(i, 1)
                    sp.wait_ge(stored[1], V_STORES + 16 * KT // 2 * (i - 1))
                    sp.dma_start(xT_now[:, :, :], xT[i - 1]).then_inc(xT_loaded, 16)
                if not tail:
                    if not first:
                        sp.wait_ge(o_mm, i * NG)
                    sp.dma_start(v_now[0:NK, :], v_scr[i, 0:NK]).then_inc(v_loaded, 16)
                if not tail and not is_at(i, LAST):
                    sp.wait_ge(s_ready, i * SLOTS + 2 * QT)
                    load_k(i + 1, 0)
                if tail:
                    for m in range(2, 4):
                        load_weights(m)
                if first:
                    for b in range(CB):
                        store_v(CB + b)
                    for s in range(2):
                        sp.wait_ge(stored[s], V_STORES)
                else:
                    for m in range(KT):
                        sp.wait_ge(x2_evac, (i - 1) * KT + m + 1)
                        sp.dma_start(x2_scr[i - 1, m], x2_out[:, m % 2, :]).then_inc(stored[m % 2], 16)

            sp.wait_ge(w_lo_done["q"], 1)
            each_batch(sp, batch)

            for m in range(4, FT):
                load_weights(m)
            for s in range(2):
                sp.wait_ge(stored[s], X2_STORES)
            sp.wait_ge(attn_done, 4)

            def keep_residual(b):
                sp.wait_ge(x2_split, (b + 1) * KT)
                sp.dma_start(x2_res[:, :, :], x2_in[:, :, :]).then_inc(res_ready, 16)

            def store_y(b):
                for m in range(KT):
                    sp.wait_ge(y_done, b * KT + m + 1)
                    sp.dma_start(yT[b, m], y_out[:, m, :]).then_inc(stored[m % 2], 16)

            keep_residual(0)
            with sp.Fori(1, B) as b:
                sp.wait_ge(res_ready, 16 * b)
                sp.dma_start(x2_in[:, :, :], x2_scr[b].rearrange("k p n -> p k n")).then_inc(x2_loaded, 16)
                store_y(b - 1)
                keep_residual(b)
            store_y(B - 1)
            for s in range(2):
                sp.wait_ge(stored[s], Y_STORES)

        @block.gpsimd
        def _(pool):
            pool.memset(ident[:, :], 0.0).then_inc(ident_zero, 1)
            pool.wait_ge(ident_zero, 1)
            pool.affine_select(out=ident[:, :], in_=ident[:, :], compare_op=ALU.not_equal, fill=1.0, base=0,
                               pattern=[[-1, P]], channel_multiplier=1).then_inc(ident_ready, 1)
            pool.memset(k_diag[:, :, :, :].bitcast(F32), 0.0).then_inc(k_zero, 1)

            def inverse_deviation(rows, unit):
                pool.wait_ge(aggregated, unit + 1)
                pool.tensor_tensor(var_eps[0:rows, :], mean_var[0:rows, :, 1], eps[0:rows, :], ALU.add).then_inc(var_done, 1)
                pool.wait_ge(var_done, unit + 1)
                pool.tensor_tensor(rstd[0:rows, :], var_eps[0:rows, :], minus_half[0:rows, :], ALU.pow).then_inc(rstd_done, 1)

            pool.memset(eps[:, :], EPS).then_inc(consts_ready, 1)
            pool.memset(minus_half[:, :], -0.5).then_inc(consts_ready, 1)
            pool.wait_ge(consts_ready, 2)
            inverse_deviation(NK, 0)
            for k in range(KT):
                pool.wait_ge(w_hi_done["k"], k + 1)
                pool.tensor_tensor(wk_lo[:, k, :], raw_a[:, k, :], wk_hi[:, k, :].bitcast(F32), ALU.subtract).then_inc(w_lo_done["k"], 1)
            inverse_deviation(NK, 1)
            for n, raw, hi, lo in (("v", raw_b, wv_hi, wv_lo), ("q", raw_a, wq_hi, wq_lo), ("o", raw_b, wo_hi, wo_lo)):
                pool.wait_ge(w_hi_done[n], 1)
                pool.tensor_tensor(lo[:, :, :], raw[:, :, :], hi[:, :, :].bitcast(F32), ALU.subtract).then_inc(w_lo_done[n], 1)
                if n == "q":
                    inverse_deviation(P, 2)

            def batch(i):
                if is_at(i, TAIL):
                    return
                for s in range(SLOTS):
                    g, t = divmod(s, QT)
                    pool.wait_ge(inv_done, i * SLOTS + s + 1)
                    p = probs[:, g % 2, t, :].rearrange("p (h n) -> p h n", h=GH)
                    inv = row_inv[:, g % 2, t * GH:(t + 1) * GH].unsqueeze(2).broadcast_to([P, GH, NK])
                    last = pool.tensor_tensor(p, p, inv, ALU.mult)
                    last.then_inc(norm_done, 1)
                    if s == LN_SLOT + QT and not is_at(i, LAST):
                        inverse_deviation(P, i + CHUNKS + 1)
                    k = s - LNT_SLOT - 1
                    if 0 <= k < KT and not is_at(i, LAST):
                        pool.wait_ge(xhi_done, (i + CHUNKS + 1) * KT + k + 1)
                        pool.tensor_tensor(xn_lo[:, k, :], x_f[:, k % 2, :], xn_hi[:, k, :].bitcast(F32), ALU.subtract).then_inc(xn_ready, 1)

            each_batch(pool, batch)
            pool.wait_ge(norm_done, B * SLOTS)
            pool.sem_inc(attn_done, 1)


        @block.tensor
        def _(pe):
            def product(out, hi, lo, moving_hi, moving_lo, start, stop):
                pe.matmul(out, hi, moving_hi, start=start, stop=False)
                pe.matmul(out, lo, moving_hi, start=False, stop=False)
                return pe.matmul(out, hi, moving_lo, start=False, stop=stop)

            def transposes(src, rows, unit, k):
                if is_at(k, 0) or k == 0:
                    pe.wait_ge(ln_done, unit + 1)
                if not (is_at(unit, 0) and k == 0):
                    pe.wait_ge(xf_done, unit * KT + k)
                for t in range(QT):
                    mm = pe.transpose(ln_bank[:, t * rows:(t + 1) * rows], src[:, t, k * P:(k + 1) * P], ident[0:rows, 0:rows])
                mm.then_inc(lnt_ready, 1)

            def q_unit(m, k):
                return product(proj[m % 2][:, :], wq_hi[:, k, m * P:(m + 1) * P], wq_lo[:, k, m * P:(m + 1) * P],
                               xn_hi[:, k, :], xn_lo[:, k, :], k == 0, k == KT - 1)

            pe.wait_ge(ident_ready, 1)
            def k_units(c, k):
                hi, lo = cn[c]
                for g in range(NG):
                    mm = product(k_bank[g][:, 0:CTOK], wk_hi[:, k, g * P:(g + 1) * P], wk_lo[:, k, g * P:(g + 1) * P],
                                 hi[:, k, 0:CTOK], lo[:, k, 0:CTOK], k == 0, k == KT - 1)
                    if k == KT - 1:
                        mm.then_inc(k_mm, 1)

            def v_unit(c, b, k, out):
                hi, lo = cn[c]
                tok = slice(b * NK, (b + 1) * NK)
                mm = product(out[0:NK, :], hi[:, k, tok], lo[:, k, tok], wv_hi[:, k, :], wv_lo[:, k, :], k == 0, k == KT - 1)
                if k == KT - 1:
                    mm.then_inc(v_mm, 1)

            transposes(ctx_tok[0], NK, 0, 0)
            for k in range(KT):
                if k + 1 < KT:
                    transposes(ctx_tok[0], NK, 0, k + 1)
                pe.wait_ge(w_lo_done["k"], k + 1)
                pe.wait_ge(xn_ready, k + 1)
                k_units(0, k)
            pe.wait_ge(w_lo_done["v"], 1)
            for b in range(CB):
                if b >= 2:
                    pe.wait_ge(v_evac, b - 1)
                for k in range(KT):
                    v_unit(0, b, k, v_bank[b % 2])
                transposes(ctx_tok[1], NK, 1, b)
            pe.wait_ge(k_evac, NG)
            for k in range(KT):
                transposes(x_tok, P, 2, k)
                pe.wait_ge(xn_ready, KT + k + 1)
                k_units(1, k)
            pe.wait_ge(w_lo_done["q"], 1)
            pe.wait_ge(k_evac, NG + 1)
            for k in range(KT):
                pe.wait_ge(xn_ready, CHUNKS * KT + k + 1)
                mm = q_unit(0, k)
            mm.then_inc(q_mm, 1)
            pe.wait_ge(k_evac, NG + 2)
            for m, k in units(Q_NEXT, max(Q_NEXT)):
                q_unit(m, k)

            def hidden_tile(b, m):
                w1_hi, w1_lo, _, _ = ffn_w[m]
                if is_at(b, 0):
                    pe.wait_ge(wlo2_done, m + 1)
                if not (is_at(b, 0) and m < 4):
                    pe.wait_ge(silu_done, b * FT + m - 3)
                for k in range(KT):
                    if m == 0:
                        pe.wait_ge(x2_split, b * KT + k + 1)
                    mm = product(acc1[m % 4][:, :], w1_hi[:, k * P:(k + 1) * P], w1_lo[:, k * P:(k + 1) * P],
                                 x2_hi[:, k, :], x2_lo[:, k, :], k == 0, k == KT - 1)
                mm.then_inc(f1_mm, 1)

            def batch(i):
                first, last, tail = is_at(i, FIRST), is_at(i, LAST), is_at(i, TAIL)

                def q_units(todo, of):
                    for m, k in todo:
                        if k == 0 and m == 0:
                            if first:
                                pe.wait_ge(v_evac, CB + 3)
                            else:
                                pe.wait_ge(x2_evac, (of - 2) * KT + 3)
                            pe.wait_ge(xn_ready, (of + CHUNKS + 1) * KT)
                        elif k == 0 and m == 1:
                            if first:
                                pe.wait_ge(v_evac, CB + 4)
                            else:
                                pe.wait_ge(x2_evac, (of - 1) * KT)
                        elif k == 0:
                            pe.wait_ge(q_ready, of * NG + m - 1)
                        mm = q_unit(m, k)
                        if k == KT - 1:
                            mm.then_inc(q_mm, 1)

                for s in range(SLOTS):
                    g, t = divmod(s, QT)
                    n = i * SLOTS + s
                    if not tail:
                        if t == 0:
                            pe.wait_ge(q_ready, i * NG + g + 1)
                            if g % 2 == 0:
                                pe.wait_ge(k_loaded[g // 2], (i + 1) * GH * 16)
                        if first and s < 2:
                            pe.wait_ge(k_evac, NG + 3 + s)
                        else:
                            pe.wait_ge(exp_done, n - 1)
                        rows = slice(t * P, (t + 1) * P)
                        product(s_bank[s % 2][:, 0:GH * NK], q_hi[:, g, rows], q_lo[:, g, rows],
                                k_diag[:, g, 0, :], k_diag[:, g, 1, :], True, True).then_inc(s_ready, 1)
                    if not (first and s < T_LAG) and not (tail and s >= T_LAG):
                        h = (s - T_LAG) % GH
                        gg = ((s - T_LAG) % SLOTS) // GH
                        if h == 0:
                            pe.wait_ge(norm_done, n - T_LAG + GH)
                        if not (first and s < T_LAG + 2):
                            pe.wait_ge(pt_ready, n - T_LAG - 1)
                        for tt in range(QT):
                            mm = pe.transpose(t_bank[s % 2][0:NK, tt * P:(tt + 1) * P],
                                              probs[:, gg % 2, tt, h * NK:(h + 1) * NK], ident[:, :])
                        mm.then_inc(t_ready, 1)
                    if s in PV_STEP and not (first and PV_STEP[s] > 1) and not (tail and PV_STEP[s] < 2):
                        gg = PV_STEP[s]
                        done = i * NG + gg - (NG if gg > 1 else 0)
                        pe.wait_ge(pt_ready, done * GH + GH)
                        if gg == 0:
                            pe.wait_ge(v_loaded, 16 * (i + 1))
                        if not (first and gg == 0):
                            pe.wait_ge(o_ready, done)
                        for h in range(GH):
                            head = gg * GH + h
                            mm = pe.matmul(o_bank[h * HD:(h + 1) * HD, :], v_now[0:NK, head * HD:(head + 1) * HD],
                                           probs_t[0:NK, (gg % 2) * GH + h, :], start=True, stop=True)
                        mm.then_inc(o_mm, 1)
                    if not tail:
                        q_units(units(Q_NOW, s, sum(Q_NEXT.values())), i)
                    if first:
                        for m, k in units(WO_BEFORE, s):
                            if k == 0 and m < 2:
                                pe.wait_ge(q_ready, 3 + m)
                            elif k == 0:
                                pe.wait_ge(v_evac, CB + m - 1)
                            v_unit(1, m, k, proj[m % 2])
                    for m, k in units(WO_BEFORE, s) if not first else ():
                        if m == 0:
                            pe.wait_ge(o_ready, (i - 1) * NG + k + 1)
                        if k == 0:
                            if m >= 2:
                                pe.wait_ge(x2_evac, (i - 1) * KT + m - 1)
                            elif tail:
                                pe.wait_ge(x2_evac, (i - 2) * KT + 3 + m)
                            else:
                                pe.wait_ge(q_ready, i * NG + 3 + m)
                        mm = product(proj[m % 2][:, :], wo_hi[:, k, m * P:(m + 1) * P], wo_lo[:, k, m * P:(m + 1) * P],
                                     o_hi[:, k, :], o_lo[:, k, :], k == 0, k == KT - 1)
                        if k == KT - 1:
                            mm.then_inc(wo_mm, 1)
                    if not tail and not last:
                        q_units(units(Q_NEXT, s), i + 1)
                    if not tail and not last and LNT_SLOT <= s < LNT_SLOT + KT:
                        transposes(x_tok, P, i + CHUNKS + 1, s - LNT_SLOT)
                    if tail and s in TAIL_HIDDEN:
                        if s == min(TAIL_HIDDEN):
                            pe.wait_ge(exp_done, B * SLOTS)
                        hidden_tile(0, TAIL_HIDDEN[s])

            pe.wait_ge(w_lo_done["o"], 1)
            each_batch(pe, batch)

            def ffn(b):
                first = is_at(b, 0)
                for m in range(FT + 1):
                    if m < FT and not (first and m < 2):
                        hidden_tile(b, m)
                    if m > 0:
                        f = m - 1
                        _, _, w2_hi, w2_lo = ffn_w[f]
                        pe.wait_ge(h_ready, b * FT + f + 1)
                        for o in range(KT):
                            if f == 0 and not first:
                                pe.wait_ge(y_done, (b - 1) * KT + o + 1)
                            elif f == 0 and o >= 2:
                                pe.wait_ge(x2_evac, B * KT - 3 + o)
                            mm = product(acc2[o][:, :], w2_hi[:, o * P:(o + 1) * P], w2_lo[:, o * P:(o + 1) * P],
                                         h_hi[:, f % 2, :], h_lo[:, f % 2, :], f == 0, f == FT - 1)
                            if f == FT - 1:
                                mm.then_inc(f2_mm, 1)

            ffn(0)
            with pe.Fori(1, B) as b:
                ffn(b)

        @block.scalar
        def _(act):
            def split(n, raw, hi):
                act.wait_ge(w_loaded[n], 16)
                act.activation(hi[:, :, :], raw[:, :, :], ACT.Copy).then_inc(w_hi_done[n], 1)

            act.wait_ge(w_loaded["k"], 16)
            for k in range(KT):
                act.activation(wk_hi[:, k, :], raw_a[:, k, :], ACT.Copy).then_inc(w_hi_done["k"], 1)
            act.wait_ge(vec_loaded, 16)
            for k in range(KT):
                if k == 2:
                    split("v", raw_b, wv_hi)
                if k >= 2:
                    act.wait_ge(xn_ready, k - 1)
                act.wait_ge(lnt_ready, k + 1)
                act.activation(x_f[:, k % 2, 0:CTOK], ln_bank[:, 0:CTOK], ACT.Identity, scale=vec[:, V_GK + k:V_GK + k + 1],
                               bias=vec[:, V_BK + k:V_BK + k + 1]).then_inc(xf_done, 1)
            split("q", raw_a, wq_hi)

            def v_out_tile(n, place):
                act.wait_ge(v_mm, n + 1)
                if n >= 2:
                    act.wait_ge(stored[n % 2], 16 * (n // 2))
                act.activation(v_out[0:NK, n % 2, :], place[n % 2][0:NK, :], ACT.Copy).then_inc(v_evac, 1)

            for c in range(CHUNKS):
                for g in range(NG):
                    act.wait_ge(k_mm, c * NG + g + 1)
                    act.activation(k_out[c][:, :, g, 0, :], k_bank[g][:, 0:CTOK].rearrange("p (b n) -> p b n", b=CB), ACT.Copy).then_inc(khi_done, 1)
                if c == 0:
                    split("o", raw_b, wo_hi)
                    for b in range(CB):
                        v_out_tile(b, v_bank)

            def q_out(m, of):
                act.wait_ge(q_mm, of * NG + m + 1)
                act.activation(q_hi[:, m, :], proj[m % 2][:, :], ACT.Copy, scale=SCALE).then_inc(qhi_done, 1)

            q_out(0, 0)
            act.wait_ge(w_lo_done["o"], 1)

            def split2(m):
                if m == Q_OVER:
                    act.wait_ge(attn_done, 4)
                act.wait_ge(wraw_loaded[m % 2], 32 * (m // 2 + 1))
                w1_hi, _, w2_hi, _ = ffn_w[m]
                act.activation(w1_hi[:, :], w_raw[:, m % 2, 0, :], ACT.Copy)
                act.activation(w2_hi[:, :], w_raw[:, m % 2, 1, :], ACT.Copy).then_inc(whi2_done, 1)

            def hidden(b, m):
                act.wait_ge(f1_mm, b * FT + m + 1)
                if not (is_at(b, 0) and m < 2):
                    act.wait_ge(h_ready, b * FT + m - 1)
                act.activation(h_f[:, m % 2, :], acc1[m % 4][:, :], ACT.Silu, bias=vec[:, V_B1 + m:V_B1 + m + 1]).then_inc(silu_done, 1)

            def batch(i):
                first, last, tail = is_at(i, FIRST), is_at(i, LAST), is_at(i, TAIL)
                for s in range(SLOTS):
                    g, t = divmod(s, QT)
                    n = i * SLOTS + s
                    if s in Q_EVAC and not tail:
                        if Q_EVAC[s] > 0:
                            q_out(Q_EVAC[s], i)
                        elif not last:
                            q_out(0, i + 1)
                    if first and s in X2_EVAC:
                        v_out_tile(CB + X2_EVAC[s], proj)
                    if s in OUT_STEP and not (first and OUT_STEP[s] > 1) and not (tail and OUT_STEP[s] < 2):
                        gg = OUT_STEP[s]
                        act.wait_ge(o_mm, i * NG + gg + 1 - (NG if gg > 1 else 0))
                        if gg == 0 and first:
                            act.wait_ge(v_mm, B)
                        elif gg == 0:
                            act.wait_ge(wo_mm, i * KT)
                        act.activation(o_hi[:, gg, :], o_bank[:, :], ACT.Copy).then_inc(ohi_done, 1)
                    if not tail:
                        act.wait_ge(max_done, n + 1)
                        if t == 0 and not (first and g < 2):
                            act.wait_ge(t_ready, n - 4)
                        for h in range(GH):
                            c = t * GH + h
                            e = act.activation(probs[:, g % 2, t, h * NK:(h + 1) * NK], s_bank[s % 2][:, h * NK:(h + 1) * NK], ACT.Exp,
                                               bias=neg_max[:, g % 2, c:c + 1], accum_out=row_sum[:, g % 2, c:c + 1])
                        e.then_inc(exp_done, 1)
                    if not (first and s < T_LAG) and not (tail and s >= T_LAG):
                        h = (s - T_LAG) % GH
                        gg = ((s - T_LAG) % SLOTS) // GH
                        act.wait_ge(t_ready, n - T_LAG + 1)
                        if h == 0 and not (first and gg < 2):
                            act.wait_ge(o_mm, i * NG + (s - T_LAG) // GH - 1)
                        if first and s == T_LAG:
                            act.wait_ge(k_stored[1], K_STORES)
                        act.activation(probs_t[0:NK, (gg % 2) * GH + h, :], t_bank[s % 2][0:NK, :], ACT.Copy).then_inc(pt_ready, 1)
                    if last and s in LAST_W_HI:
                        split2(LAST_W_HI[s])
                    if tail and s in TAIL_SILU:
                        hidden(0, TAIL_SILU[s])
                    if tail and s in TAIL_W_HI:
                        split2(TAIL_W_HI[s])

            each_batch(act, batch)
            act.wait_ge(ohi_done, B * NG)
            act.sem_inc(attn_done, 1)

            for m in range(2, FT):
                hidden(0, m)
                if m + 2 < FT:
                    split2(m + 2)
            with act.Fori(1, B) as b:
                for m in range(FT):
                    hidden(b, m)

        @block.vector
        def _(dve):
            def ln_stats(src, rows, t):
                dve.bn_stats(stats[0:rows, t, :], src[:, t, :]).then_inc(stats_step, 1)

            def ln_aggregate(rows):
                for t in range(QT):
                    ins = dve.bn_aggr(mean_var[0:rows, t, :], stats[0:rows, t, :])
                ins.then_inc(aggregated, 1)

            def ln_apply(src, rows, unit):
                dve.wait_ge(rstd_done, unit + 1)
                for t in range(QT):
                    ins = dve.tensor_scalar(src[:, t, :], src[:, t, :], mean_var[0:rows, t, 0:1], rstd[0:rows, t:t + 1],
                                            ALU.subtract, ALU.mult)
                ins.then_inc(ln_done, 1)

            def ln_out(unit, k, width, hi, lo, v_g, v_b):
                if not is_at(unit, 0):
                    dve.wait_ge(xn_ready, unit * KT + k - 1)
                    dve.wait_ge(lnt_ready, unit * KT + k + 1)
                    dve.tensor_scalar(x_f[:, k % 2, 0:width], ln_bank[:, 0:width], vec[:, v_g + k:v_g + k + 1], vec[:, v_b + k:v_b + k + 1],
                                      ALU.mult, ALU.add).then_inc(xf_done, 1)
                dve.wait_ge(xf_done, unit * KT + k + 1)
                dve.tensor_copy(hi[:, k, 0:width], x_f[:, k % 2, 0:width]).then_inc(xhi_done, 1)
                if isinstance(unit, int) and unit <= CHUNKS:
                    dve.wait_ge(xhi_done, unit * KT + k + 1)
                    dve.tensor_tensor(lo[:, k, 0:width], x_f[:, k % 2, 0:width], hi[:, k, 0:width].bitcast(F32), ALU.subtract).then_inc(xn_ready, 1)

            def q_low(m, of):
                dve.wait_ge(qhi_done, of * NG + m + 1)
                dve.scalar_tensor_tensor(q_lo[:, m, :], proj[m % 2][:, :], SCALE, q_hi[:, m, :].bitcast(F32),
                                         ALU.mult, ALU.subtract).then_inc(q_ready, 1)

            def ln_statistics(src, rows, unit):
                for t in range(QT):
                    if unit == 0:
                        dve.wait_ge(ctx0_loaded[t], 16)
                    ln_stats(src, rows, t)
                dve.wait_ge(stats_step, (unit + 1) * QT)
                ln_aggregate(rows)

            def k_low(c):
                for g in range(NG):
                    dve.wait_ge(khi_done, c * NG + g + 1)
                    dve.tensor_tensor(k_out[c][:, :, g, 1, :], k_bank[g][:, 0:CTOK].rearrange("p (b n) -> p b n", b=CB), k_out[c][:, :, g, 0, :].bitcast(F32),
                                      ALU.subtract).then_inc(k_evac, 1)

            ln_statistics(ctx_tok[0], NK, 0)
            ln_apply(ctx_tok[0], NK, 0)
            for k in range(KT):
                if k == 2:
                    dve.wait_ge(ctx1_loaded, 16)
                    ln_statistics(ctx_tok[1], NK, 1)
                ln_out(0, k, CTOK, *cn[0], V_GK, V_BK)
            ln_apply(ctx_tok[1], NK, 1)
            dve.wait_ge(x_loaded, 16)
            ln_statistics(x_tok, P, 2)
            k_low(0)
            ln_apply(x_tok, P, 2)
            dve.wait_ge(vec_loaded, 16)
            for k in range(KT):
                ln_out(1, k, CTOK, *cn[1], V_GK, V_BK)
            dve.wait_ge(k_stored[0], K_STORES)
            for k in range(KT):
                ln_out(2, k, NQ, xn_hi, xn_lo, V_GQ, V_BQ)
            k_low(1)
            q_low(0, 0)

            def split2(m):
                dve.wait_ge(whi2_done, m + 1)
                w1_hi, w1_lo, w2_hi, w2_lo = ffn_w[m]
                dve.tensor_tensor(w1_lo[:, :], w_raw[:, m % 2, 0, :], w1_hi[:, :].bitcast(F32), ALU.subtract)
                dve.tensor_tensor(w2_lo[:, :], w_raw[:, m % 2, 1, :], w2_hi[:, :].bitcast(F32), ALU.subtract).then_inc(wlo2_done, 1)

            def split_x2(b, k):
                if k == 0:
                    dve.wait_ge(x2_loaded, 16 * (b + 1))
                    if not is_at(b, 0):
                        dve.wait_ge(f1_mm, b * FT)
                dve.tensor_copy(x2_hi[:, k, :], x2_in[:, k, :]).then_inc(x2hi_done, 1)
                dve.wait_ge(x2hi_done, b * KT + k + 1)
                dve.tensor_tensor(x2_lo[:, k, :], x2_in[:, k, :], x2_hi[:, k, :].bitcast(F32), ALU.subtract).then_inc(x2_split, 1)

            def hidden(b, m):
                dve.wait_ge(silu_done, b * FT + m + 1)
                dve.tensor_copy(h_hi[:, m % 2, :], h_f[:, m % 2, :]).then_inc(hhi_done, 1)
                dve.wait_ge(hhi_done, b * FT + m + 1)
                dve.tensor_tensor(h_lo[:, m % 2, :], h_f[:, m % 2, :], h_hi[:, m % 2, :].bitcast(F32), ALU.subtract).then_inc(h_ready, 1)

            def inverse(n, g, t):
                dve.wait_ge(exp_done, n + 1)
                c = slice(t * GH, (t + 1) * GH)
                dve.reciprocal(row_inv[:, g % 2, c], row_sum[:, g % 2, c]).then_inc(inv_done, 1)

            def batch(i):
                first, last, tail = is_at(i, FIRST), is_at(i, LAST), is_at(i, TAIL)
                for s in range(SLOTS):
                    g, t = divmod(s, QT)
                    n = i * SLOTS + s
                    aggregate = not tail and not last and s == LN_SLOT + QT
                    if aggregate:
                        dve.wait_ge(stats_step, (i + CHUNKS + 2) * QT)
                    if not tail:
                        dve.wait_ge(s_ready, n + 1)
                        c = slice(t * GH, (t + 1) * GH)
                        dve.tensor_reduce(neg_max[:, g % 2, c], s_bank[s % 2][:, 0:GH * NK].rearrange("p (h n) -> p h n", h=GH),
                                          AX.X, ALU.max, negate=True).then_inc(max_done, 1)
                    if aggregate:
                        ln_aggregate(P)
                    if not (first and s == 0) and not (tail and s > 0):
                        pg, pt = divmod((s - 1) % SLOTS, QT)
                        inverse(n - 1, pg, pt)
                    if s in OUT_STEP and not (first and OUT_STEP[s] > 1) and not (tail and OUT_STEP[s] < 2):
                        gg = OUT_STEP[s]
                        dve.wait_ge(ohi_done, i * NG + gg + 1 - (NG if gg > 1 else 0))
                        dve.tensor_tensor(o_lo[:, gg, :], o_bank[:, :], o_hi[:, gg, :].bitcast(F32), ALU.subtract).then_inc(o_ready, 1)
                    if s in Q_EVAC and not tail:
                        if Q_EVAC[s] > 0:
                            q_low(Q_EVAC[s], i)
                        elif not last:
                            q_low(0, i + 1)
                    if not tail and not last:
                        if LN_SLOT <= s < LN_SLOT + QT:
                            if s == LN_SLOT:
                                dve.wait_ge(x_loaded, 16 * (i + 2))
                            ln_stats(x_tok, P, s - LN_SLOT)
                        if s == LN_APPLY:
                            ln_apply(x_tok, P, i + CHUNKS + 1)
                        if LNT_SLOT + 1 <= s < LNT_SLOT + 1 + KT:
                            ln_out(i + CHUNKS + 1, s - LNT_SLOT - 1, NQ, xn_hi, xn_lo, V_GQ, V_BQ)
                    if not first and s in X2_EVAC:
                        m = X2_EVAC[s]
                        dve.wait_ge(wo_mm, (i - 1) * KT + m + 1)
                        if m == 0:
                            dve.wait_ge(xT_loaded, 16 * i)
                        dve.wait_ge(stored[m % 2], V_STORES + 16 * KT // 2 * (i - 1) + 16 * (m // 2))
                        dve.scalar_tensor_tensor(x2_out[:, m % 2, :], proj[m % 2][:, :], vec[:, V_BO + m:V_BO + m + 1], xT_now[:, m, :],
                                                 ALU.add, ALU.add).then_inc(x2_evac, 1)
                    if last and s in X2_SPLIT:
                        split_x2(0, X2_SPLIT[s])
                    if last and s in LAST_W_LO:
                        split2(LAST_W_LO[s])
                    if tail and s in TAIL_H:
                        hidden(0, TAIL_H[s])
                    if tail and s in TAIL_W_LO:
                        split2(TAIL_W_LO[s])

            each_batch(dve, batch)
            dve.wait_ge(x2_evac, B * KT)
            dve.sem_inc(attn_done, 2)

            def finish(b):
                dve.wait_ge(res_ready, 16 * (b + 1))
                for s in range(2):
                    dve.wait_ge(stored[s], X2_STORES + 16 * KT // 2 * b)
                for o in range(KT):
                    dve.wait_ge(f2_mm, b * KT + o + 1)
                    dve.scalar_tensor_tensor(y_out[:, o, :], acc2[o][:, :], vec[:, V_B2 + o:V_B2 + o + 1], x2_res[:, o, :],
                                             ALU.add, ALU.add).then_inc(y_done, 1)

            for m in range(2, FT):
                hidden(0, m)
                if m + 2 < FT:
                    split2(m + 2)
            with dve.Fori(1, B) as b:
                for k in range(KT):
                    split_x2(b, k)
                finish(b - 1)
                for m in range(FT):
                    hidden(b, m)
            finish(B - 1)


def kernel(**inputs):
    import numpy as np
    import concourse.bacc as bacc
    from concourse.bass_utils import run_bass_kernel_spmd as run

    a = {k.removeprefix("L0_xattn_"): np.asarray(v) for k, v in inputs.items()}

    def cols(v):
        return v.reshape(-1, P).T

    c = np.ascontiguousarray
    wkv = a["Wkv"]
    arrays = {
        "in_x": c(a["x"]),
        "in_xT": c(a["x"].reshape(B, NQ, KT, P).transpose(0, 3, 2, 1)),
        "in_ctx": c(a["ctx_1024"].reshape(B * NK, D)),
        "in_wqT": c(a["Wq"].T),
        "in_wkT": c(wkv[0:D].T),
        "in_wvT": c(wkv[D:2 * D].T),
        "in_woT": c(a["Wo"].T),
        "in_w1": c(a["W1"].reshape(FT, P, KT, P).transpose(0, 3, 2, 1).reshape(FT, P, KT * P)),
        "in_w2": c(a["W2"].T.reshape(FT, P, D)),
        "in_vecs": c(np.concatenate([cols(a[n]) for n in ("ln_q_g", "ln_q_b", "ln_kv_g", "ln_kv_b", "bo", "b2", "b1")], axis=1)),
    }
    nc = bacc.Bacc("TRN2", target_bir_lowering=False, num_devices=1)
    args = [nc.dram_tensor(n, v.shape, mybir.dt.from_np(v.dtype), kind="ExternalInput").ap() for n, v in arrays.items()]
    args.append(nc.dram_tensor("out_y", (B, KT, P, NQ), F32, kind="ExternalOutput").ap())
    cross_attention_block(nc, *args)
    y = run(nc, [arrays], core_ids=[0]).results[0]["out_y"]
    return y.transpose(0, 3, 1, 2).reshape(B, NQ, D)
```

```python
from contextlib import ExitStack

import concourse.bass as bass
from concourse import mybir

F32 = mybir.dt.float32
F32R = mybir.dt.float32r
ALU = mybir.AluOpType
ACT = mybir.ActivationFunctionType
AX = mybir.AxisListType

P = 128
B, NQ, D = 8, 512, 512
NK = 120
H, HD = 16, 32
DFF = 4 * D
KT = D // P
GH = P // HD
NG = H // GH
QT = NQ // P
FT = DFF // P
CB = 4
CHUNKS = B // CB
CTOK = CB * NK
SCALE = float(HD) ** -0.5
EPS = 1e-5
V_GQ, V_BQ, V_GK, V_BK, V_BO, V_B2, V_B1 = 0, KT, 2 * KT, 3 * KT, 4 * KT, 5 * KT, 6 * KT
NV = 6 * KT + FT

WARM_UP = 11

SLOTS = NG * QT
T_LAG = 5
PT_ON_DVE = (1, 3, 5, 15)
PV_STEP = {9: 0, 14: 1, 1: 2, 5: 3}
OUT_STEP = {13: 0, 15: 1, 2: 2, 6: 3}
LN_SLOT = 0
LN_APPLY = 6
LNT_SLOT = 7
LN_OUT_STEP = {7: 0, 9: 1, 10: 2, 11: 3}
Q_NEXT = {13: 2, 14: 2, 15: 2}
Q_NOW = {0: 2, 1: 2, 2: 2, 3: 2, 4: 2}
WO_BEFORE = {5: 2, 6: 1, 7: 2, 8: 2, 9: 2, 10: 2, 11: 2, 12: 3}
Q_HI_STEP = {1: 1, 3: 2, 5: 3, 15: 0}
Q_LO_STEP = {1: 1, 4: 2, 5: 3, 15: 0}
X2_EVAC = {8: 0, 10: 1, 12: 2, 13: 3}

X2_SPLIT = {8: 0, 9: 1, 10: 2, 11: 3}
LAST_W_HI, LAST_W_LO = {8: 0, 10: 1}, {12: 0, 14: 1}
LAST_HIDDEN = {13: 2, 14: 2, 15: 2}
TAIL_HIDDEN = {0: 2, 5: 4}
TAIL_SILU = {0: 0, 1: 1}
TAIL_H = {4: 0, 6: 1}
TAIL_W_HI, TAIL_W_LO = {2: 2, 4: 3}, {3: 2, 5: 3}
TAIL_WO = {2: 2, 3: 2, 4: 2, 6: 2, 7: 2, 8: 2, 9: 2, 10: 2}
TAIL_WO_ORDER = [(m, k) for k in range(KT) for m in (0, 1)] + [(m, k) for m in (2, 3) for k in range(KT)]


def units(table, step, skip=0):
    done = skip + sum(n for s, n in table.items() if s < step)
    return [divmod(done + j, KT) for j in range(table.get(step, 0))]


def moved_out(i, head):
    on_dve = [(s - T_LAG) % SLOTS for s in PT_ON_DVE]
    by_dve = len([h for h in on_dve if h <= head])
    return i * (SLOTS - len(on_dve)) + head + 1 - by_dve, i * len(on_dve) + by_dve


def cross_attention_block(nc, x, xT, ctx_in, wqT, wkT, wvT, woT, w1c, w2c, vecs, yT):
    k_scr = nc.dram_tensor("k_scratch", [B, P, NG, 2, NK], F32).ap()
    v_scr = nc.dram_tensor("v_scratch", [B, P, D], F32).ap()
    x2_scr = nc.dram_tensor("x2_scratch", [B, KT, P, NQ], F32).ap()

    with ExitStack() as outer:
        def sem(name):
            return outer.enter_context(nc.semaphore(name))

        vec = outer.enter_context(nc.sbuf_tensor("vec", [P, NV], F32))
        bank = [outer.enter_context(nc.psum_tensor(f"bank{i}", [P, 512], F32)) for i in range(8)]

        def placed(place, name, shape, dt=F32):
            return place.enter_context(nc.sbuf_tensor(name, shape, dt))

        def weights(m, place):
            return [placed(place, f"{n}_{m}", [P, 512], F32R) for n in ("w1_hi", "w1_lo", "w2_hi", "w2_lo")]

        ffn_w = [weights(0, outer)]

        early = ExitStack()

        def sb(name, shape, dt=F32):
            return early.enter_context(nc.sbuf_tensor(name, shape, dt))

        wk_hi, wk_lo = sb("wk_hi", [P, KT, D], F32R), sb("wk_lo", [P, KT, D], F32R)
        wv_hi, wv_lo = sb("wv_hi", [P, KT, D], F32R), sb("wv_lo", [P, KT, D], F32R)
        wq_hi, wq_lo = sb("wq_hi", [P, KT, D], F32R), sb("wq_lo", [P, KT, D], F32R)
        x_tok = sb("x_tok", [P, QT, D])
        xn = sb("xn", [P, 2, KT, NQ], F32R)
        xn_hi, xn_lo = xn[:, 0, :, :], xn[:, 1, :, :]
        q_pair = sb("q_pair", [P, NG, 2, NQ], F32R)
        k_pair = sb("k_pair", [P, NG, 2, 2, 2 * NK], F32R)
        wo_hi, wo_lo = sb("wo_hi", [P, KT, D], F32R), sb("wo_lo", [P, KT, D], F32R)
        ident = sb("ident", [P, P])
        stats = sb("stats", [P, QT, 6])
        mean_var = sb("mean_var", [P, QT, 2])
        eps, var_eps, minus_half, rstd = (sb(n, [P, QT]) for n in ("eps", "var_eps", "minus_half", "rstd"))
        x_f = sb("x_f", [P, 2, NQ])
        o_hi, o_lo = sb("o_hi", [P, KT, NQ], F32R), sb("o_lo", [P, KT, NQ], F32R)
        v_now = sb("v_now", [P, D])
        probs = sb("probs", [P, 2, QT, GH * NK])
        probs_t = sb("probs_t", [P, 2 * GH, NQ])
        neg_max = sb("neg_max", [P, 2, QT * GH])
        row_sum = sb("row_sum", [P, 2, QT * GH])
        row_inv = sb("row_inv", [P, 2, QT * GH])
        xT_now = sb("xT_now", [P, KT, NQ])
        x2_out = sb("x2_out", [P, 2, NQ])
        early.close()

        late = ExitStack()
        outer.enter_context(late)

        def sl(name, shape, dt=F32):
            return late.enter_context(nc.sbuf_tensor(name, shape, dt))

        w_raw = sl("w_raw", [P, 2, 2, 512])
        x2_in = sl("x2_in", [P, KT, NQ])
        x2_hi, x2_lo = sl("x2_hi", [P, KT, NQ], F32R), sl("x2_lo", [P, KT, NQ], F32R)
        ffn_w += [weights(m, late) for m in range(1, 4)]
        h_f = sl("h_f", [P, 2, NQ])
        h_hi, h_lo = sl("h_hi", [P, 2, NQ], F32R), sl("h_lo", [P, 2, NQ], F32R)
        Q_OVER = 7
        ffn_w += [weights(m, late) for m in range(4, Q_OVER)]
        x2_res = sl("x2_res", [P, KT, NQ])
        ffn_w += [weights(m, late) for m in range(Q_OVER, FT)]

        y_out = w_raw[:, :, :, :].rearrange("p a b n -> p (a b) n")

        raw_a = xT_now
        raw_b = probs[:, :, :, :].rearrange("p a t n -> p (a t n)")[:, 0:KT * D].rearrange("p (k n) -> p k n", k=KT)
        ctx_tok = [probs_t[0:NK, c * CB:(c + 1) * CB, :] for c in range(CHUNKS)]
        cn = [(q_pair[:, :, 0, :], q_pair[:, :, 1, :]), (o_hi, o_lo)]
        k_out = [place[:, 0:CB * NG * 2 * NK].rearrange("p (b g t n) -> p b g t n", b=CB, g=NG, t=2)
                 for place in (xn[:, :, :, :].rearrange("p a k n -> p (a k n)"),
                               probs_t[:, :, :].rearrange("p h n -> p (h n)").bitcast(F32R))]
        v_out = x2_out

        k_bank, v_bank = [bank[1], bank[2], bank[3], bank[4]], bank[5:7]
        ln_bank, proj, s_bank, t_bank, o_bank = bank[0], bank[1:3], bank[3:5], bank[5:7], bank[7]
        acc2 = [bank[0], bank[7], bank[1], bank[2]]
        acc1 = [bank[5], bank[6], bank[3], bank[4]]
        acc1_start = [bank[0], bank[1]]

        def hidden_bank(b, m):
            return acc1_start[m] if isinstance(b, int) and b == 0 and m < 2 else acc1[m % 4]

        vec_loaded, ident_zero, ident_ready, consts_ready, k_zero = sem("vec_loaded"), sem("ident_zero"), sem("ident_ready"), sem("consts_ready"), sem("k_zero")
        ctx0_loaded, ctx1_loaded = [sem(f"ctx0_loaded{t}") for t in range(CB)], sem("ctx1_loaded")
        x_loaded, xT_loaded, v_loaded = sem("x_loaded"), sem("xT_loaded"), sem("v_loaded")
        k_loaded = [sem("k01_loaded"), sem("k23_loaded")]
        w_loaded = {n: sem(f"w{n}_loaded") for n in "kvqo"}
        w_hi_done = {n: sem(f"w{n}_hi_done") for n in "kvqo"}
        w_lo_done = {n: sem(f"w{n}_lo_done") for n in "kvqo"}
        k_stored = [sem(f"k_stored{c}") for c in range(CHUNKS)]
        K_STORES = 16
        stored = [sem("stored0"), sem("stored1")]
        V_STORES = 16 * B // 2
        X2_STORES = V_STORES + 16 * B * KT // 2
        Y_STORES = X2_STORES + 16 * B * KT // 2
        stats_step, aggregated, var_done, rstd_done, ln_done = sem("stats_step"), sem("aggregated"), sem("var_done"), sem("rstd_done"), sem("ln_done")
        lnt_ready, xf_done, xhi_done, xn_ready = sem("lnt_ready"), sem("xf_done"), sem("xhi_done"), sem("xn_ready")
        k_mm, v_mm, q_mm, wo_mm = sem("k_mm"), sem("v_mm"), sem("q_mm"), sem("wo_mm")
        khi_done, k_evac, v_evac = sem("khi_done"), sem("k_evac"), sem("v_evac")
        qhi_done, q_ready, x2_evac = sem("qhi_done"), sem("q_ready"), sem("x2_evac")
        s_ready, max_done, exp_done, inv_done, norm_done = (sem(n) for n in ("s_ready", "max_done", "exp_done", "inv_done", "norm_done"))
        t_ready, o_mm, ohi_done, o_ready = (sem(n) for n in ("t_ready", "o_mm", "ohi_done", "o_ready"))
        pt_act, pt_dve = sem("pt_act"), sem("pt_dve")
        attn_done = sem("attn_done")
        wraw_loaded, whi2_done, wlo2_done = [sem("wraw_loaded0"), sem("wraw_loaded1")], sem("whi2_done"), sem("wlo2_done")
        x2_loaded, x2hi_done, x2_split, res_ready = sem("x2_loaded"), sem("x2hi_done"), sem("x2_split"), sem("res_ready")
        h0_used = sem("h0_used")
        f1_mm, silu_done, hhi_done, h_ready, f2_mm, y_done = (sem(n) for n in ("f1_mm", "silu_done", "hhi_done", "h_ready", "f2_mm", "y_done"))

        FIRST, LAST, TAIL = 0, B - 1, B

        def is_at(i, n):
            return isinstance(i, int) and i == n

        def probs_t_place(eng, i, s):
            head = (s - T_LAG) % SLOTS
            g, h = divmod(head, GH)
            eng.wait_ge(t_ready, i * SLOTS + s - T_LAG + 1)
            if not (is_at(i, FIRST) and g < 2):
                eng.wait_ge(o_mm, i * NG + (s - T_LAG) // GH - 1)
            elif s < T_LAG + 2:
                eng.wait_ge(k_stored[1], K_STORES)
            return probs_t[0:NK, (g % 2) * GH + h, :], t_bank[s % 2][0:NK, :]

        def each_batch(eng, step):
            step(FIRST)
            with eng.Fori(1, LAST) as i:
                step(i)
            step(LAST)
            step(TAIL)

        block = outer.enter_context(nc.Block())

        @block.sync
        def _(sp):
            for t in range(CB):
                sp.dma_start(ctx_tok[0][:, t, :], ctx_in[t * NK:(t + 1) * NK, :]).then_inc(ctx0_loaded[t], 16)
            sp.dma_start(raw_a[:, :, :], wkT.rearrange("(k p) n -> p k n", p=P)).then_inc(w_loaded["k"], 16)
            sp.dma_start(vec[:, :], vecs).then_inc(vec_loaded, 16)
            sp.dma_start(raw_b, wvT.rearrange("(k p) n -> p k n", p=P)).then_inc(w_loaded["v"], 16)
            sp.dma_start(ctx_tok[1], ctx_in[CTOK:2 * CTOK, :].rearrange("(t p) d -> p t d", p=NK)).then_inc(ctx1_loaded, 16)
            sp.dma_start(x_tok[:, :, :], x[0].rearrange("(t p) d -> p t d", p=P)).then_inc(x_loaded, 16)
            sp.wait_ge(w_lo_done["k"], KT)
            sp.dma_start(raw_a[:, :, :], wqT.rearrange("(k p) n -> p k n", p=P)).then_inc(w_loaded["q"], 16)
            sp.wait_ge(w_lo_done["v"], 1)
            sp.dma_start(raw_b, woT.rearrange("(k p) n -> p k n", p=P)).then_inc(w_loaded["o"], 16)

            def load_x(b):
                sp.wait_ge(lnt_ready, (b + CHUNKS) * KT)
                sp.dma_start(x_tok[:, :, :], x[b].rearrange("(t p) d -> p t d", p=P)).then_inc(x_loaded, 16)

            def load_k(b, half):
                groups = slice(2 * half, 2 * half + 2)
                for j in range(GH):
                    pair, e = divmod(j, 2)
                    for top in (HD * e, P // 2 + HD * e):
                        sp.dma_start(k_pair[top:top + HD, groups, :, pair, e * NK:(e + 1) * NK].bitcast(F32),
                                     k_scr[b, HD * j:HD * (j + 1), groups, :, :]).then_inc(k_loaded[half], 16)

            def store_v(b):
                sp.wait_ge(v_evac, b + 1)
                sp.dma_start(v_scr[b, 0:NK], v_out[0:NK, b % 2, :]).then_inc(stored[b % 2], 16)

            for c in range(CHUNKS):
                if c == 1:
                    load_x(1)
                sp.wait_ge(k_evac, (c + 1) * NG)
                sp.dma_start(k_scr[c * CB:(c + 1) * CB].rearrange("b p g t n -> p b (g t n)"),
                             k_out[c].bitcast(F32).rearrange("p b g t n -> p b (g t n)")).then_inc(k_stored[c], 16)
                if c == 0:
                    for b in range(CB):
                        store_v(b)
                    sp.wait_ge(k_stored[0], K_STORES)
                    sp.wait_ge(k_zero, 1)
                    load_k(0, 0)
                    load_k(0, 1)
            sp.wait_ge(k_stored[1], K_STORES)
            for s in range(2):
                sp.wait_ge(stored[s], V_STORES // CHUNKS)

            def load_weights(m):
                if m >= 2:
                    sp.wait_ge(wlo2_done, m - 1)
                sp.dma_start(w_raw[:, m % 2, 0, :], w1c[m]).then_inc(wraw_loaded[m % 2], 16)
                sp.dma_start(w_raw[:, m % 2, 1, :], w2c[m]).then_inc(wraw_loaded[m % 2], 16)

            def batch(i):
                first, tail = is_at(i, FIRST), is_at(i, TAIL)
                if is_at(i, LAST):
                    for s in range(2):
                        sp.wait_ge(stored[s], V_STORES + 16 * KT // 2)
                    sp.dma_start(x2_in[:, :, :], x2_scr[0].rearrange("k p n -> p k n")).then_inc(x2_loaded, 16)
                    load_weights(0)
                    load_weights(1)
                if not first and not tail and not is_at(i, LAST):
                    load_x(i + 1)
                if not first:
                    if not tail:
                        sp.wait_ge(s_ready, i * SLOTS)
                        load_k(i, 1)
                    sp.wait_ge(stored[1], V_STORES + 16 * KT // 2 * (i - 1))
                    sp.dma_start(xT_now[:, :, :], xT[i - 1]).then_inc(xT_loaded, 16)
                if not tail:
                    if not first:
                        sp.wait_ge(o_mm, i * NG)
                    sp.dma_start(v_now[0:NK, :], v_scr[i, 0:NK]).then_inc(v_loaded, 16)
                if not tail and not is_at(i, LAST):
                    sp.wait_ge(s_ready, i * SLOTS + 2 * QT)
                    load_k(i + 1, 0)
                if tail:
                    for m in range(2, 4):
                        load_weights(m)
                if first:
                    for b in range(CB):
                        store_v(CB + b)
                    for s in range(2):
                        sp.wait_ge(stored[s], V_STORES)
                else:
                    for m in range(KT):
                        sp.wait_ge(x2_evac, (i - 1) * KT + m + 1)
                        sp.dma_start(x2_scr[i - 1, m], x2_out[:, m % 2, :]).then_inc(stored[m % 2], 16)

            sp.wait_ge(w_lo_done["q"], 1)
            each_batch(sp, batch)

            for m in range(4, FT):
                load_weights(m)
            for s in range(2):
                sp.wait_ge(stored[s], X2_STORES)
            sp.wait_ge(attn_done, 4)

            def keep_residual(b):
                sp.wait_ge(x2_split, (b + 1) * KT)
                sp.dma_start(x2_res[:, :, :], x2_in[:, :, :]).then_inc(res_ready, 16)

            def store_y(b):
                for m in range(KT):
                    sp.wait_ge(y_done, b * KT + m + 1)
                    sp.dma_start(yT[b, m], y_out[:, m, :]).then_inc(stored[m % 2], 16)

            keep_residual(0)
            with sp.Fori(1, B) as b:
                sp.wait_ge(res_ready, 16 * b)
                sp.dma_start(x2_in[:, :, :], x2_scr[b].rearrange("k p n -> p k n")).then_inc(x2_loaded, 16)
                store_y(b - 1)
                keep_residual(b)
            store_y(B - 1)
            for s in range(2):
                sp.wait_ge(stored[s], Y_STORES)

        @block.gpsimd
        def _(pool):
            pool.memset(ident[:, :], 0.0).then_inc(ident_zero, 1)
            pool.wait_ge(ident_zero, 1)
            pool.affine_select(out=ident[:, :], in_=ident[:, :], compare_op=ALU.not_equal, fill=1.0, base=0,
                               pattern=[[-1, P]], channel_multiplier=1).then_inc(ident_ready, 1)
            pool.memset(k_pair[:, :, :, :, :].bitcast(F32), 0.0).then_inc(k_zero, 1)

            def inverse_deviation(rows, unit):
                pool.wait_ge(aggregated, unit + 1)
                pool.tensor_tensor(var_eps[0:rows, :], mean_var[0:rows, :, 1], eps[0:rows, :], ALU.add).then_inc(var_done, 1)
                pool.wait_ge(var_done, unit + 1)
                pool.tensor_tensor(rstd[0:rows, :], var_eps[0:rows, :], minus_half[0:rows, :], ALU.pow).then_inc(rstd_done, 1)

            pool.memset(eps[:, :], EPS).then_inc(consts_ready, 1)
            pool.memset(minus_half[:, :], -0.5).then_inc(consts_ready, 1)
            pool.wait_ge(consts_ready, 2)
            inverse_deviation(NK, 0)
            for k in range(KT):
                pool.wait_ge(w_hi_done["k"], k + 1)
                pool.tensor_tensor(wk_lo[:, k, :], raw_a[:, k, :], wk_hi[:, k, :].bitcast(F32), ALU.subtract).then_inc(w_lo_done["k"], 1)
            inverse_deviation(NK, 1)
            for n, raw, hi, lo in (("v", raw_b, wv_hi, wv_lo), ("q", raw_a, wq_hi, wq_lo), ("o", raw_b, wo_hi, wo_lo)):
                pool.wait_ge(w_hi_done[n], 1)
                pool.tensor_tensor(lo[:, :, :], raw[:, :, :], hi[:, :, :].bitcast(F32), ALU.subtract).then_inc(w_lo_done[n], 1)
                if n == "q":
                    inverse_deviation(P, 2)

            def batch(i):
                if is_at(i, TAIL):
                    return
                for s in range(SLOTS):
                    g, t = divmod(s, QT)
                    pool.wait_ge(inv_done, i * SLOTS + s + 1)
                    p = probs[:, g % 2, t, :].rearrange("p (h n) -> p h n", h=GH)
                    inv = row_inv[:, g % 2, t * GH:(t + 1) * GH].unsqueeze(2).broadcast_to([P, GH, NK])
                    pool.tensor_tensor(p, p, inv, ALU.mult).then_inc(norm_done, 1)
                    if s == LN_SLOT + QT and not is_at(i, LAST):
                        inverse_deviation(P, i + CHUNKS + 1)
                    if s in LN_OUT_STEP and not is_at(i, LAST):
                        k = LN_OUT_STEP[s]
                        pool.wait_ge(xhi_done, (i + CHUNKS + 1) * KT + k + 1)
                        pool.tensor_tensor(xn_lo[:, k, :], x_f[:, k % 2, :], xn_hi[:, k, :].bitcast(F32), ALU.subtract).then_inc(xn_ready, 1)

            each_batch(pool, batch)
            pool.wait_ge(norm_done, B * SLOTS)
            pool.sem_inc(attn_done, 1)

        @block.tensor
        def _(pe):
            def product(out, hi, lo, moving_hi, moving_lo, start, stop):
                pe.matmul(out, hi, moving_hi, start=start, stop=False)
                pe.matmul(out, lo, moving_hi, start=False, stop=False)
                return pe.matmul(out, hi, moving_lo, start=False, stop=stop)

            def transposes(src, rows, unit, k):
                if k == 0:
                    pe.wait_ge(ln_done, unit + 1)
                if not (is_at(unit, 0) and k == 0):
                    pe.wait_ge(xf_done, unit * KT + k)
                for t in range(QT):
                    mm = pe.transpose(ln_bank[:, t * rows:(t + 1) * rows], src[:, t, k * P:(k + 1) * P], ident[0:rows, 0:rows])
                mm.then_inc(lnt_ready, 1)

            def q_unit(m, k, out=None):
                return product((out or proj[m % 2])[:, :], wq_hi[:, k, m * P:(m + 1) * P], wq_lo[:, k, m * P:(m + 1) * P],
                               xn_hi[:, k, :], xn_lo[:, k, :], k == 0, k == KT - 1)

            def k_units(c, k):
                hi, lo = cn[c]
                for g in range(NG):
                    mm = product(k_bank[g][:, 0:CTOK], wk_hi[:, k, g * P:(g + 1) * P], wk_lo[:, k, g * P:(g + 1) * P],
                                 hi[:, k, 0:CTOK], lo[:, k, 0:CTOK], k == 0, k == KT - 1)
                    if k == KT - 1:
                        mm.then_inc(k_mm, 1)

            def v_unit(c, b, k, out):
                hi, lo = cn[c]
                tok = slice(b * NK, (b + 1) * NK)
                mm = product(out[0:NK, :], hi[:, k, tok], lo[:, k, tok], wv_hi[:, k, :], wv_lo[:, k, :], k == 0, k == KT - 1)
                if k == KT - 1:
                    mm.then_inc(v_mm, 1)

            pe.wait_ge(ident_ready, 1)
            with pe.Fori(0, WARM_UP):
                for t in range(QT):
                    pe.transpose(v_bank[0][:, t * P:(t + 1) * P], ident[:, :], ident[:, :])
            transposes(ctx_tok[0], NK, 0, 0)
            for k in range(KT):
                if k + 1 < KT:
                    transposes(ctx_tok[0], NK, 0, k + 1)
                pe.wait_ge(w_lo_done["k"], k + 1)
                pe.wait_ge(xn_ready, k + 1)
                k_units(0, k)
            pe.wait_ge(w_lo_done["v"], 1)
            for b in range(CB):
                if b >= 2:
                    pe.wait_ge(v_evac, b - 1)
                for k in range(KT):
                    v_unit(0, b, k, v_bank[b % 2])
                transposes(ctx_tok[1], NK, 1, b)
            pe.wait_ge(k_evac, NG)
            for k in range(KT):
                pe.wait_ge(xn_ready, KT + k + 1)
                k_units(1, k)
                transposes(x_tok, P, 2, k)

            pe.wait_ge(w_lo_done["q"], 1)
            pe.wait_ge(v_evac, CB - 1)
            for k in range(KT):
                pe.wait_ge(xn_ready, CHUNKS * KT + k + 1)
                mm = q_unit(0, k, v_bank[0])
            mm.then_inc(q_mm, 1)
            pe.wait_ge(k_evac, NG + 2)
            for m, k in units(Q_NEXT, max(Q_NEXT)):
                q_unit(m, k)

            def hidden_unit(b, m, k):
                w1_hi, w1_lo, _, _ = ffn_w[m]
                if k == 0:
                    if is_at(b, 0):
                        pe.wait_ge(wlo2_done, m + 1)
                    if not (is_at(b, 0) and m < 4):
                        pe.wait_ge(silu_done, b * FT + m - 3)
                if m == 0:
                    pe.wait_ge(x2_split, b * KT + k + 1)
                mm = product(hidden_bank(b, m)[:, :], w1_hi[:, k * P:(k + 1) * P], w1_lo[:, k * P:(k + 1) * P],
                             x2_hi[:, k, :], x2_lo[:, k, :], k == 0, k == KT - 1)
                if k == KT - 1:
                    mm.then_inc(f1_mm, 1)

            def batch(i):
                first, last, tail = is_at(i, FIRST), is_at(i, LAST), is_at(i, TAIL)

                def q_units(todo, of):
                    for m, k in todo:
                        if k == 0 and m == 0:
                            if first:
                                pe.wait_ge(v_evac, CB + 3)
                            else:
                                pe.wait_ge(x2_evac, (of - 2) * KT + 3)
                            pe.wait_ge(xn_ready, (of + CHUNKS + 1) * KT)
                        elif k == 0 and m == 1:
                            if first:
                                pe.wait_ge(v_evac, CB + 4)
                            else:
                                pe.wait_ge(x2_evac, (of - 1) * KT)
                        elif k == 0:
                            pe.wait_ge(q_ready, of * NG + m - 1)
                        mm = q_unit(m, k)
                        if k == KT - 1:
                            mm.then_inc(q_mm, 1)

                def scores(s):
                    if tail:
                        return
                    g, t = divmod(s, QT)
                    n = i * SLOTS + s
                    if t == 0:
                        pe.wait_ge(q_ready, i * NG + g + 1)
                        if g % 2 == 0:
                            pe.wait_ge(k_loaded[g // 2], (i + 1) * 2 * GH * 16)
                    if first and s < 2:
                        pe.wait_ge(k_evac, NG + 3 + s)
                    else:
                        pe.wait_ge(exp_done, n - 1)
                    rows = slice(t * P, (t + 1) * P)
                    for pair in range(2):
                        for part in range(2):
                            mm = pe.matmul(s_bank[s % 2][:, pair * 2 * NK:(pair + 1) * 2 * NK], q_pair[:, g, pair, rows],
                                           k_pair[:, g, part, pair, :], start=(part == 0), stop=(part == 1))
                    mm.then_inc(s_ready, 1)

                def transposes_of_head(s):
                    n = i * SLOTS + s
                    if not (first and s < T_LAG) and not (tail and s >= T_LAG):
                        h = (s - T_LAG) % GH
                        gg = ((s - T_LAG) % SLOTS) // GH
                        if h == 0:
                            pe.wait_ge(norm_done, n - T_LAG + GH)
                        if not (first and s < T_LAG + 2):
                            batch_before, head = divmod(s - 2 - T_LAG, SLOTS)
                            by_act, by_dve = moved_out(i + batch_before, head)
                            if (s - 2) % SLOTS in PT_ON_DVE:
                                pe.wait_ge(pt_dve, by_dve)
                            else:
                                pe.wait_ge(pt_act, by_act)
                        for tt in range(QT):
                            mm = pe.transpose(t_bank[s % 2][0:NK, tt * P:(tt + 1) * P],
                                              probs[:, gg % 2, tt, h * NK:(h + 1) * NK], ident[:, :])
                        mm.then_inc(t_ready, 1)

                def times_v(s):
                    if s in PV_STEP and not (first and PV_STEP[s] > 1) and not (tail and PV_STEP[s] < 2):
                        gg = PV_STEP[s]
                        done = i * NG + gg - (NG if gg > 1 else 0)
                        by_act, by_dve = moved_out(i - (1 if gg > 1 else 0), gg * GH + GH - 1)
                        pe.wait_ge(pt_act, by_act)
                        pe.wait_ge(pt_dve, by_dve)
                        if gg == 0:
                            pe.wait_ge(v_loaded, 16 * (i + 1))
                        if not (first and gg == 0):
                            pe.wait_ge(o_ready, done)
                        for h in range(GH):
                            head = gg * GH + h
                            mm = pe.matmul(o_bank[h * HD:(h + 1) * HD, :], v_now[0:NK, head * HD:(head + 1) * HD],
                                           probs_t[0:NK, (gg % 2) * GH + h, :], start=True, stop=True)
                        mm.then_inc(o_mm, 1)

                for s in range(SLOTS):
                    for part in (transposes_of_head, scores) if s == 0 else (scores, transposes_of_head):
                        if tail and part == transposes_of_head:
                            times_v(s)
                        part(s)
                    if tail and s in TAIL_HIDDEN:
                        for m, k in units(TAIL_HIDDEN, s, sum(LAST_HIDDEN.values())):
                            if m == 2 and k == 0:
                                pe.wait_ge(exp_done, B * SLOTS)
                            hidden_unit(0, m, k)
                    if not tail:
                        q_units(units(Q_NOW, s, sum(Q_NEXT.values())), i)
                    if first:
                        for m, k in units(WO_BEFORE, s):
                            if k == 0 and m < 2:
                                pe.wait_ge(q_ready, 3 + m)
                            elif k == 0:
                                pe.wait_ge(v_evac, CB + m - 1)
                            v_unit(1, m, k, proj[m % 2])
                    todo = units(WO_BEFORE, s) if not tail else [TAIL_WO_ORDER[m * KT + k] for m, k in units(TAIL_WO, s)]
                    for m, k in todo if not first else ():
                        if m == 0:
                            pe.wait_ge(o_ready, (i - 1) * NG + k + 1)
                        if k == 0:
                            if m >= 2:
                                pe.wait_ge(x2_evac, (i - 1) * KT + m - 1)
                            elif tail:
                                pe.wait_ge(silu_done, 2)
                                pe.wait_ge(x2_evac, (i - 2) * KT + 3 + m)
                            else:
                                pe.wait_ge(q_ready, i * NG + 3 + m)
                        mm = product(proj[m % 2][:, :], wo_hi[:, k, m * P:(m + 1) * P], wo_lo[:, k, m * P:(m + 1) * P],
                                     o_hi[:, k, :], o_lo[:, k, :], k == 0, k == KT - 1)
                        if k == KT - 1:
                            mm.then_inc(wo_mm, 1)
                    if not tail and not last:
                        q_units(units(Q_NEXT, s), i + 1)
                    if not tail:
                        times_v(s)
                    if not tail and not last and LNT_SLOT <= s < LNT_SLOT + KT:
                        transposes(x_tok, P, i + CHUNKS + 1, s - LNT_SLOT)
                    if last:
                        for m, k in units(LAST_HIDDEN, s):
                            if (m, k) == (1, 0):
                                pe.wait_ge(x2_evac, (i - 1) * KT + 3)
                            hidden_unit(0, m, k)

            pe.wait_ge(w_lo_done["o"], 1)
            each_batch(pe, batch)

            def ffn(b):
                first = is_at(b, 0)
                for m in range(FT + 1):
                    if m < FT and not (first and m < 3):
                        for k in range(KT):
                            hidden_unit(b, m, k)
                    if m > 0:
                        f = m - 1
                        _, _, w2_hi, w2_lo = ffn_w[f]
                        pe.wait_ge(h_ready, b * FT + f + 1)
                        for o in range(KT):
                            if f == 0 and not first:
                                pe.wait_ge(y_done, (b - 1) * KT + o + 1)
                            elif f == 0 and o >= 2:
                                pe.wait_ge(x2_evac, B * KT - 3 + o)
                            mm = product(acc2[o][:, :], w2_hi[:, o * P:(o + 1) * P], w2_lo[:, o * P:(o + 1) * P],
                                         h_hi[:, f % 2, :], h_lo[:, f % 2, :], f == 0, f == FT - 1)
                            if f == FT - 1:
                                mm.then_inc(f2_mm, 1)
                        if first and f == 0:
                            mm.then_inc(h0_used, 1)

            ffn(0)
            with pe.Fori(1, B) as b:
                ffn(b)

        @block.scalar
        def _(act):
            def split(n, raw, hi):
                act.wait_ge(w_loaded[n], 16)
                act.activation(hi[:, :, :], raw[:, :, :], ACT.Copy).then_inc(w_hi_done[n], 1)

            act.wait_ge(w_loaded["k"], 16)
            for k in range(KT):
                act.activation(wk_hi[:, k, :], raw_a[:, k, :], ACT.Copy).then_inc(w_hi_done["k"], 1)
            act.wait_ge(vec_loaded, 16)
            for k in range(KT):
                if k == 2:
                    split("v", raw_b, wv_hi)
                if k >= 2:
                    act.wait_ge(xn_ready, k - 1)
                act.wait_ge(lnt_ready, k + 1)
                act.activation(x_f[:, k % 2, 0:CTOK], ln_bank[:, 0:CTOK], ACT.Identity, scale=vec[:, V_GK + k:V_GK + k + 1],
                               bias=vec[:, V_BK + k:V_BK + k + 1]).then_inc(xf_done, 1)
            split("q", raw_a, wq_hi)

            def v_out_tile(n, place):
                act.wait_ge(v_mm, n + 1)
                if n >= 2:
                    act.wait_ge(stored[n % 2], 16 * (n // 2))
                act.activation(v_out[0:NK, n % 2, :], place[n % 2][0:NK, :], ACT.Copy).then_inc(v_evac, 1)

            for c in range(CHUNKS):
                for g in range(NG):
                    act.wait_ge(k_mm, c * NG + g + 1)
                    act.activation(k_out[c][:, :, g, 0, :], k_bank[g][:, 0:CTOK].rearrange("p (b n) -> p b n", b=CB),
                                   ACT.Copy).then_inc(khi_done, 1)
                if c == 0:
                    split("o", raw_b, wo_hi)
                    for b in range(CB):
                        v_out_tile(b, v_bank)

            def q_out(m, of, place=proj):
                act.wait_ge(q_mm, of * NG + m + 1)
                for pair in range(2):
                    act.activation(q_pair[0:P // 2, m, pair, :], place[m % 2][pair * P // 2:(pair + 1) * P // 2, :], ACT.Copy,
                                   scale=SCALE).then_inc(qhi_done, 1)

            q_out(0, 0, v_bank)
            act.wait_ge(w_lo_done["o"], 1)

            def split2(m):
                if m == Q_OVER:
                    act.wait_ge(attn_done, 4)
                act.wait_ge(wraw_loaded[m % 2], 32 * (m // 2 + 1))
                w1_hi, _, w2_hi, _ = ffn_w[m]
                act.activation(w1_hi[:, :], w_raw[:, m % 2, 0, :], ACT.Copy)
                act.activation(w2_hi[:, :], w_raw[:, m % 2, 1, :], ACT.Copy).then_inc(whi2_done, 1)

            def hidden(b, m):
                act.wait_ge(f1_mm, b * FT + m + 1)
                if not (is_at(b, 0) and m < 2):
                    act.wait_ge(h_ready, b * FT + m - 1)
                act.activation(h_f[:, m % 2, :], hidden_bank(b, m)[:, :], ACT.Silu, bias=vec[:, V_B1 + m:V_B1 + m + 1]).then_inc(silu_done, 1)

            def batch(i):
                first, last, tail = is_at(i, FIRST), is_at(i, LAST), is_at(i, TAIL)
                for s in range(SLOTS):
                    g, t = divmod(s, QT)
                    n = i * SLOTS + s
                    if s in Q_HI_STEP and s in Q_LO_STEP:
                        if Q_HI_STEP[s] > 0 and not tail:
                            q_out(Q_HI_STEP[s], i)
                        elif Q_HI_STEP[s] == 0 and not tail and not last:
                            q_out(0, i + 1)
                    if first and s in X2_EVAC:
                        v_out_tile(CB + X2_EVAC[s], proj)
                    if s in OUT_STEP and not (first and OUT_STEP[s] > 1) and not (tail and OUT_STEP[s] < 2):
                        gg = OUT_STEP[s]
                        act.wait_ge(o_mm, i * NG + gg + 1 - (NG if gg > 1 else 0))
                        if gg == 0 and first:
                            act.wait_ge(v_mm, B)
                        elif gg == 0:
                            act.wait_ge(wo_mm, i * KT)
                        act.activation(o_hi[:, gg, :], o_bank[:, :], ACT.Copy).then_inc(ohi_done, 1)
                    if not tail:
                        act.wait_ge(max_done, n + 1)
                        if t == 0 and not (first and g < 2):
                            act.wait_ge(t_ready, n - 4)
                        for h in range(GH):
                            c = t * GH + h
                            e = act.activation(probs[:, g % 2, t, h * NK:(h + 1) * NK], s_bank[s % 2][:, h * NK:(h + 1) * NK], ACT.Exp,
                                               bias=neg_max[:, g % 2, c:c + 1], accum_out=row_sum[:, g % 2, c:c + 1])
                        e.then_inc(exp_done, 1)
                        if s in Q_HI_STEP and s not in Q_LO_STEP:
                            q_out(Q_HI_STEP[s], i)
                    if s not in PT_ON_DVE and not (first and s < T_LAG) and not (tail and s >= T_LAG):
                        place, ready = probs_t_place(act, i, s)
                        act.activation(place, ready, ACT.Copy).then_inc(pt_act, 1)
                    if last and s in LAST_W_HI:
                        split2(LAST_W_HI[s])
                    if tail and s in TAIL_SILU:
                        hidden(0, TAIL_SILU[s])
                    if tail and s in TAIL_W_HI:
                        split2(TAIL_W_HI[s])

            each_batch(act, batch)
            act.wait_ge(ohi_done, B * NG)
            act.sem_inc(attn_done, 1)

            for m in range(2, FT):
                hidden(0, m)
                if m + 2 < FT:
                    split2(m + 2)
            with act.Fori(1, B) as b:
                for m in range(FT):
                    hidden(b, m)

        @block.vector
        def _(dve):
            def ln_stats(src, rows, t):
                dve.bn_stats(stats[0:rows, t, :], src[:, t, :]).then_inc(stats_step, 1)

            def ln_aggregate(rows):
                for t in range(QT):
                    ins = dve.bn_aggr(mean_var[0:rows, t, :], stats[0:rows, t, :])
                ins.then_inc(aggregated, 1)

            def ln_apply(src, rows, unit):
                dve.wait_ge(rstd_done, unit + 1)
                for t in range(QT):
                    ins = dve.tensor_scalar(src[:, t, :], src[:, t, :], mean_var[0:rows, t, 0:1], rstd[0:rows, t:t + 1],
                                            ALU.subtract, ALU.mult)
                ins.then_inc(ln_done, 1)

            def ln_out(unit, k, width, hi, lo, v_g, v_b):
                if not is_at(unit, 0):
                    dve.wait_ge(xn_ready, unit * KT + k - 1)
                    dve.wait_ge(lnt_ready, unit * KT + k + 1)
                    dve.tensor_scalar(x_f[:, k % 2, 0:width], ln_bank[:, 0:width], vec[:, v_g + k:v_g + k + 1], vec[:, v_b + k:v_b + k + 1],
                                      ALU.mult, ALU.add).then_inc(xf_done, 1)
                dve.wait_ge(xf_done, unit * KT + k + 1)
                dve.tensor_copy(hi[:, k, 0:width], x_f[:, k % 2, 0:width]).then_inc(xhi_done, 1)
                if isinstance(unit, int) and unit <= CHUNKS:
                    dve.wait_ge(xhi_done, unit * KT + k + 1)
                    dve.tensor_tensor(lo[:, k, 0:width], x_f[:, k % 2, 0:width], hi[:, k, 0:width].bitcast(F32), ALU.subtract).then_inc(xn_ready, 1)

            def q_low(m, of, place=proj):
                for pair in range(2):
                    dve.wait_ge(qhi_done, 2 * (of * NG + m) + pair + 1)
                    ins = dve.scalar_tensor_tensor(q_pair[P // 2:P, m, pair, :], place[m % 2][pair * P // 2:(pair + 1) * P // 2, :], SCALE,
                                                   q_pair[0:P // 2, m, pair, :].bitcast(F32), ALU.mult, ALU.subtract)
                ins.then_inc(q_ready, 1)

            def ln_statistics(src, rows, unit):
                for t in range(QT):
                    if unit == 0:
                        dve.wait_ge(ctx0_loaded[t], 16)
                    ln_stats(src, rows, t)
                dve.wait_ge(stats_step, (unit + 1) * QT)
                ln_aggregate(rows)

            def k_low(c, groups):
                for g in groups:
                    dve.wait_ge(khi_done, c * NG + g + 1)
                    dve.tensor_tensor(k_out[c][:, :, g, 1, :], k_bank[g][:, 0:CTOK].rearrange("p (b n) -> p b n", b=CB),
                                      k_out[c][:, :, g, 0, :].bitcast(F32), ALU.subtract).then_inc(k_evac, 1)

            ln_statistics(ctx_tok[0], NK, 0)
            ln_apply(ctx_tok[0], NK, 0)
            for k in range(KT):
                if k == 2:
                    dve.wait_ge(ctx1_loaded, 16)
                    ln_statistics(ctx_tok[1], NK, 1)
                ln_out(0, k, CTOK, *cn[0], V_GK, V_BK)
            ln_apply(ctx_tok[1], NK, 1)
            dve.wait_ge(x_loaded, 16)
            ln_statistics(x_tok, P, 2)
            k_low(0, range(NG))
            dve.wait_ge(vec_loaded, 16)
            for k in range(KT):
                if k == 1:
                    ln_apply(x_tok, P, 2)
                ln_out(1, k, CTOK, *cn[1], V_GK, V_BK)
            dve.wait_ge(k_stored[0], K_STORES)
            for k in range(KT):
                if k == KT - 1:
                    k_low(1, range(0, 2))
                ln_out(2, k, NQ, xn_hi, xn_lo, V_GQ, V_BQ)
            k_low(1, range(2, NG))
            q_low(0, 0, v_bank)

            def split2(m):
                dve.wait_ge(whi2_done, m + 1)
                w1_hi, w1_lo, w2_hi, w2_lo = ffn_w[m]
                dve.tensor_tensor(w1_lo[:, :], w_raw[:, m % 2, 0, :], w1_hi[:, :].bitcast(F32), ALU.subtract)
                dve.tensor_tensor(w2_lo[:, :], w_raw[:, m % 2, 1, :], w2_hi[:, :].bitcast(F32), ALU.subtract).then_inc(wlo2_done, 1)

            def split_x2(b, k):
                if k == 0:
                    dve.wait_ge(x2_loaded, 16 * (b + 1))
                    if not is_at(b, 0):
                        dve.wait_ge(f1_mm, b * FT)
                dve.tensor_copy(x2_hi[:, k, :], x2_in[:, k, :]).then_inc(x2hi_done, 1)
                dve.wait_ge(x2hi_done, b * KT + k + 1)
                dve.tensor_tensor(x2_lo[:, k, :], x2_in[:, k, :], x2_hi[:, k, :].bitcast(F32), ALU.subtract).then_inc(x2_split, 1)

            def hidden(b, m):
                dve.wait_ge(silu_done, b * FT + m + 1)
                if is_at(b, 0) and m == 2:
                    dve.wait_ge(h0_used, 1)
                dve.tensor_copy(h_hi[:, m % 2, :], h_f[:, m % 2, :]).then_inc(hhi_done, 1)
                dve.wait_ge(hhi_done, b * FT + m + 1)
                dve.tensor_tensor(h_lo[:, m % 2, :], h_f[:, m % 2, :], h_hi[:, m % 2, :].bitcast(F32), ALU.subtract).then_inc(h_ready, 1)

            def inverse(n, g, t):
                dve.wait_ge(exp_done, n + 1)
                c = slice(t * GH, (t + 1) * GH)
                dve.reciprocal(row_inv[:, g % 2, c], row_sum[:, g % 2, c]).then_inc(inv_done, 1)

            def batch(i):
                first, last, tail = is_at(i, FIRST), is_at(i, LAST), is_at(i, TAIL)
                for s in range(SLOTS):
                    g, t = divmod(s, QT)
                    n = i * SLOTS + s
                    if t == 0 and not (first and s == 0) and not (tail and s > 0):
                        inverse(n - 1, (g - 1) % NG, QT - 1)
                    aggregate = not tail and not last and s == LN_SLOT + QT
                    if aggregate:
                        dve.wait_ge(stats_step, (i + CHUNKS + 2) * QT)
                    if not tail:
                        dve.wait_ge(s_ready, n + 1)
                        c = slice(t * GH, (t + 1) * GH)
                        dve.tensor_reduce(neg_max[:, g % 2, c], s_bank[s % 2][:, 0:GH * NK].rearrange("p (h n) -> p h n", h=GH),
                                          AX.X, ALU.max, negate=True).then_inc(max_done, 1)
                    if aggregate:
                        ln_aggregate(P)
                    if t > 0 and not tail:
                        inverse(n - 1, g, t - 1)
                    if not tail and not last:
                        if LN_SLOT <= s < LN_SLOT + QT:
                            if s == LN_SLOT:
                                dve.wait_ge(x_loaded, 16 * (i + 2))
                            ln_stats(x_tok, P, s - LN_SLOT)
                    if s in Q_LO_STEP and not tail:
                        if Q_LO_STEP[s] > 0:
                            q_low(Q_LO_STEP[s], i)
                        elif not last:
                            q_low(0, i + 1)
                    if s in PT_ON_DVE and not (first and s < T_LAG) and not (tail and s >= T_LAG):
                        place, ready = probs_t_place(dve, i, s)
                        dve.tensor_copy(place, ready).then_inc(pt_dve, 1)
                    if s in OUT_STEP and not (first and OUT_STEP[s] > 1) and not (tail and OUT_STEP[s] < 2):
                        gg = OUT_STEP[s]
                        dve.wait_ge(ohi_done, i * NG + gg + 1 - (NG if gg > 1 else 0))
                        dve.tensor_tensor(o_lo[:, gg, :], o_bank[:, :], o_hi[:, gg, :].bitcast(F32), ALU.subtract).then_inc(o_ready, 1)
                    if not tail and not last:
                        if s == LN_APPLY:
                            ln_apply(x_tok, P, i + CHUNKS + 1)
                        if s in LN_OUT_STEP:
                            ln_out(i + CHUNKS + 1, LN_OUT_STEP[s], NQ, xn_hi, xn_lo, V_GQ, V_BQ)
                    if not first and s in X2_EVAC:
                        m = X2_EVAC[s]
                        dve.wait_ge(wo_mm, (i - 1) * KT + m + 1)
                        if m == 0:
                            dve.wait_ge(xT_loaded, 16 * i)
                        dve.wait_ge(stored[m % 2], V_STORES + 16 * KT // 2 * (i - 1) + 16 * (m // 2))
                        dve.scalar_tensor_tensor(x2_out[:, m % 2, :], proj[m % 2][:, :], vec[:, V_BO + m:V_BO + m + 1], xT_now[:, m, :],
                                                 ALU.add, ALU.add).then_inc(x2_evac, 1)
                    if last and s in X2_SPLIT:
                        split_x2(0, X2_SPLIT[s])
                    if last and s in LAST_W_LO:
                        split2(LAST_W_LO[s])
                    if tail and s in TAIL_H:
                        hidden(0, TAIL_H[s])
                    if tail and s in TAIL_W_LO:
                        split2(TAIL_W_LO[s])

            each_batch(dve, batch)
            dve.wait_ge(x2_evac, B * KT)
            dve.sem_inc(attn_done, 2)

            def finish(b):
                dve.wait_ge(res_ready, 16 * (b + 1))
                for s in range(2):
                    dve.wait_ge(stored[s], X2_STORES + 16 * KT // 2 * b)
                for o in range(KT):
                    dve.wait_ge(f2_mm, b * KT + o + 1)
                    dve.scalar_tensor_tensor(y_out[:, o, :], acc2[o][:, :], vec[:, V_B2 + o:V_B2 + o + 1], x2_res[:, o, :],
                                             ALU.add, ALU.add).then_inc(y_done, 1)

            for m in range(2, FT):
                hidden(0, m)
                if m + 2 < FT:
                    split2(m + 2)
            with dve.Fori(1, B) as b:
                for k in range(KT):
                    split_x2(b, k)
                finish(b - 1)
                for m in range(FT):
                    hidden(b, m)
            finish(B - 1)


def kernel(**inputs):
    import numpy as np
    import concourse.bacc as bacc
    from concourse.bass_utils import run_bass_kernel_spmd as run

    a = {k.removeprefix("L0_xattn_"): np.asarray(v) for k, v in inputs.items()}

    def cols(v):
        return v.reshape(-1, P).T

    c = np.ascontiguousarray
    wkv = a["Wkv"]
    arrays = {
        "in_x": c(a["x"]),
        "in_xT": c(a["x"].reshape(B, NQ, KT, P).transpose(0, 3, 2, 1)),
        "in_ctx": c(a["ctx_1024"].reshape(B * NK, D)),
        "in_wqT": c(a["Wq"].T),
        "in_wkT": c(wkv[0:D].T),
        "in_wvT": c(wkv[D:2 * D].T),
        "in_woT": c(a["Wo"].T),
        "in_w1": c(a["W1"].reshape(FT, P, KT, P).transpose(0, 3, 2, 1).reshape(FT, P, KT * P)),
        "in_w2": c(a["W2"].T.reshape(FT, P, D)),
        "in_vecs": c(np.concatenate([cols(a[n]) for n in ("ln_q_g", "ln_q_b", "ln_kv_g", "ln_kv_b", "bo", "b2", "b1")], axis=1)),
    }
    nc = bacc.Bacc("TRN2", target_bir_lowering=False, num_devices=1)
    args = [nc.dram_tensor(n, v.shape, mybir.dt.from_np(v.dtype), kind="ExternalInput").ap() for n, v in arrays.items()]
    args.append(nc.dram_tensor("out_y", (B, KT, P, NQ), F32, kind="ExternalOutput").ap())
    cross_attention_block(nc, *args)
    y = run(nc, [arrays], core_ids=[0]).results[0]["out_y"]
    return y.transpose(0, 3, 1, 2).reshape(B, NQ, D)
```
